# Optimizing a Trainium2 kernel written in Bass

```python
import numpy as np
import jax
import jax.numpy as jnp

def _softmax(x, axis=-1):
    return jax.nn.softmax(x, axis=axis)

def _gelu(x):
    return jax.nn.gelu(x, approximate=True)

def _silu(x):
    return jax.nn.silu(x)

def _sigmoid(x):
    return jax.nn.sigmoid(x)

def _layernorm(x, axis=-1, eps=1e-05):
    m = jnp.mean(x, axis=axis, keepdims=True)
    v = jnp.var(x, axis=axis, keepdims=True)
    return (x - m) / jnp.sqrt(v + eps)

def _scatter_add(tgt, idx, src, axis=0):
    return tgt.at[idx].add(src)

def _segment_sum(src, seg, n):
    return jax.ops.segment_sum(src, seg, n)
kernel_name = 'mk_prb_d1_jaxref_r8_236b38'

def setup_inputs(seed: int=0):
    np.random.seed(seed)
    _w = jnp.asarray

    def _L0_attn_setup():
        import jax, jax.numpy as jnp
        import numpy as np
        B, S, QD = (2, 512, 256)
        H, D = (32, 64)
        INNER = H * D
        key = jax.random.key(seed)
        ks = jax.random.split(key, 6)
        scale = 1.0 / np.sqrt(QD)
        return {'hidden_states': jax.random.normal(ks[0], (B, S, QD), dtype=jnp.float32), 'Wq': jax.random.normal(ks[1], (QD, INNER), dtype=jnp.float32) * scale, 'Wk': jax.random.normal(ks[2], (QD, INNER), dtype=jnp.float32) * scale, 'Wv': jax.random.normal(ks[3], (QD, INNER), dtype=jnp.float32) * scale, 'Wo': jax.random.normal(ks[4], (INNER, QD), dtype=jnp.float32) * (1.0 / np.sqrt(INNER)), 'bo': jax.random.normal(ks[5], (QD,), dtype=jnp.float32) * 0.01}
    _L0_attn_in = _L0_attn_setup()

    def _L0_ffn_setup():
        import jax, jax.numpy as jnp
        import numpy as np
        B, S, HID = (2, 256, 256)
        NUM_HEADS = 16
        HEAD_DIM = HID // NUM_HEADS
        NUM_EXPERTS = 8
        TOP_K = 2
        INTER = 512
        EPS = 1e-05

        def _rmsnorm(x, w, eps=EPS):
            return x * jax.lax.rsqrt(jnp.mean(x * x, axis=-1, keepdims=True) + eps) * w

        def _moe(x_flat, Wr, Wg, Wu, Wd):
            T = x_flat.shape[0]
            logits = x_flat @ Wr.T
            top_logits, top_idx = jax.lax.top_k(logits, TOP_K)
            probs = jax.nn.softmax(top_logits, axis=-1)
            cw = jnp.zeros((T, NUM_EXPERTS), x_flat.dtype)
            cw = cw.at[jnp.arange(T)[:, None], top_idx].add(probs)
            hg = jnp.einsum('eih,th->eti', Wg, x_flat)
            hu = jnp.einsum('eih,th->eti', Wu, x_flat)
            y = jnp.einsum('ehi,eti->eth', Wd, jax.nn.silu(hg) * hu)
            return jnp.einsum('eth,te->th', y, cw)
        key = jax.random.key(seed)
        ks = jax.random.split(key, 12)
        sd_h = 1.0 / np.sqrt(HID)
        sd_i = 1.0 / np.sqrt(INTER)
        return {'x': jax.random.normal(ks[0], (B, S, HID), jnp.float32), 'Wq': jax.random.normal(ks[1], (HID, HID), jnp.float32) * sd_h, 'Wk': jax.random.normal(ks[2], (HID, HID), jnp.float32) * sd_h, 'Wv': jax.random.normal(ks[3], (HID, HID), jnp.float32) * sd_h, 'Wo': jax.random.normal(ks[4], (HID, HID), jnp.float32) * sd_h, 'w_ln1': jnp.ones((HID,), jnp.float32), 'w_ln2': jnp.ones((HID,), jnp.float32), 'Wr': jax.random.normal(ks[5], (NUM_EXPERTS, HID), jnp.float32) * sd_h, 'Wg': jax.random.normal(ks[6], (NUM_EXPERTS, INTER, HID), jnp.float32) * sd_h, 'Wu': jax.random.normal(ks[7], (NUM_EXPERTS, INTER, HID), jnp.float32) * sd_h, 'Wd': jax.random.normal(ks[8], (NUM_EXPERTS, HID, INTER), jnp.float32) * sd_i}
    _L0_ffn_in = _L0_ffn_setup()
    _d = {'L0_attn_hidden_states': _L0_attn_in['hidden_states'], 'L0_attn_Wq': _L0_attn_in['Wq'], 'L0_attn_Wk': _L0_attn_in['Wk'], 'L0_attn_Wv': _L0_attn_in['Wv'], 'L0_attn_Wo': _L0_attn_in['Wo'], 'L0_attn_bo': _L0_attn_in['bo'], 'L0_ffn_Wq': _L0_ffn_in['Wq'], 'L0_ffn_Wk': _L0_ffn_in['Wk'], 'L0_ffn_Wv': _L0_ffn_in['Wv'], 'L0_ffn_Wo': _L0_ffn_in['Wo'], 'L0_ffn_w_ln1': _L0_ffn_in['w_ln1'], 'L0_ffn_w_ln2': _L0_ffn_in['w_ln2'], 'L0_ffn_Wr': _L0_ffn_in['Wr'], 'L0_ffn_Wg': _L0_ffn_in['Wg'], 'L0_ffn_Wu': _L0_ffn_in['Wu'], 'L0_ffn_Wd': _L0_ffn_in['Wd']}
    _x0 = _d['L0_attn_hidden_states']
    _d['L0_attn_hidden_states'] = jax.random.normal(jax.random.fold_in(jax.random.key(seed), 1), (8, 512, 256), dtype=_x0.dtype)
    del _x0
    return _d

def reference(L0_attn_hidden_states, L0_attn_Wq, L0_attn_Wk, L0_attn_Wv, L0_attn_Wo, L0_attn_bo, L0_ffn_Wq, L0_ffn_Wk, L0_ffn_Wv, L0_ffn_Wo, L0_ffn_w_ln1, L0_ffn_w_ln2, L0_ffn_Wr, L0_ffn_Wg, L0_ffn_Wu, L0_ffn_Wd):

    def _L0_attn_ref(hidden_states, Wq, Wk, Wv, Wo, bo):
        import jax, jax.numpy as jnp
        import numpy as np
        B, S, QD = (2, 512, 256)
        H, D = (32, 64)
        INNER = H * D
        b, s, _ = hidden_states.shape

        def proj(W):
            return (hidden_states @ W).reshape(b, s, H, D).transpose(0, 2, 1, 3)
        q = jax.nn.relu(proj(Wq))
        k = jax.nn.relu(proj(Wk))
        v = proj(Wv)
        kv = jnp.einsum('bhsd,bhse->bhde', k, v)
        qkv = jnp.einsum('bhsd,bhde->bhse', q, kv)
        key_sum = k.sum(axis=2)
        normalizer = jnp.einsum('bhsd,bhd->bhs', q, key_sum)
        normalizer = jnp.clip(normalizer, 1e-06, None)[..., None]
        out = qkv / normalizer
        out = out.transpose(0, 2, 1, 3).reshape(b, s, INNER)
        return out @ Wo + bo

    def _L0_ffn_ref(x, Wq, Wk, Wv, Wo, w_ln1, w_ln2, Wr, Wg, Wu, Wd):
        import jax, jax.numpy as jnp
        import numpy as np
        B, S, HID = (2, 256, 256)
        NUM_HEADS = 16
        HEAD_DIM = HID // NUM_HEADS
        NUM_EXPERTS = 8
        TOP_K = 2
        INTER = 512
        EPS = 1e-05

        def _rmsnorm(x, w, eps=EPS):
            return x * jax.lax.rsqrt(jnp.mean(x * x, axis=-1, keepdims=True) + eps) * w

        def _moe(x_flat, Wr, Wg, Wu, Wd):
            T = x_flat.shape[0]
            logits = x_flat @ Wr.T
            top_logits, top_idx = jax.lax.top_k(logits, TOP_K)
            probs = jax.nn.softmax(top_logits, axis=-1)
            cw = jnp.zeros((T, NUM_EXPERTS), x_flat.dtype)
            cw = cw.at[jnp.arange(T)[:, None], top_idx].add(probs)
            hg = jnp.einsum('eih,th->eti', Wg, x_flat)
            hu = jnp.einsum('eih,th->eti', Wu, x_flat)
            y = jnp.einsum('ehi,eti->eth', Wd, jax.nn.silu(hg) * hu)
            return jnp.einsum('eth,te->th', y, cw)
        b, s, hid = x.shape
        residual = x
        xn = _rmsnorm(x, w_ln1)
        q = (xn @ Wq.T).reshape(b, s, NUM_HEADS, HEAD_DIM)
        k = (xn @ Wk.T).reshape(b, s, NUM_HEADS, HEAD_DIM)
        v = (xn @ Wv.T).reshape(b, s, NUM_HEADS, HEAD_DIM)
        scale = 1.0 / np.sqrt(HEAD_DIM)
        attn = jnp.einsum('bqhd,bkhd->bhqk', q, k) * scale
        causal = jnp.tril(jnp.ones((s, s), bool))
        attn = jnp.where(causal[None, None], attn, -jnp.inf)
        attn = jax.nn.softmax(attn, axis=-1)
        h = jnp.einsum('bhqk,bkhd->bqhd', attn, v).reshape(b, s, hid)
        x = residual + h @ Wo.T
        residual = x
        xn = _rmsnorm(x, w_ln2)
        moe_out = _moe(xn.reshape(-1, hid), Wr, Wg, Wu, Wd).reshape(b, s, hid)
        return residual + moe_out
    x = L0_attn_hidden_states
    xn = _layernorm(x, axis=-1)
    x = x + _L0_attn_ref(xn, L0_attn_Wq, L0_attn_Wk, L0_attn_Wv, L0_attn_Wo, L0_attn_bo) + _L0_ffn_ref(xn, L0_ffn_Wq, L0_ffn_Wk, L0_ffn_Wv, L0_ffn_Wo, L0_ffn_w_ln1, L0_ffn_w_ln2, L0_ffn_Wr, L0_ffn_Wg, L0_ffn_Wu, L0_ffn_Wd)
    return x

_drawn_inputs = setup_inputs


def setup_inputs(seed=0):
    import zlib

    import numpy as np

    out = dict(_drawn_inputs(seed))
    spreads = {'L0_ffn_w_ln1': (1.0, 0.2), 'L0_ffn_w_ln2': (1.0, 0.2)}
    factors = {'L0_attn_Wq': 6.277, 'L0_attn_Wk': 5.234, 'L0_attn_bo': 8.0}
    for name, (base, spread) in spreads.items():
        noise = np.random.default_rng([zlib.crc32(name.encode()), seed]).standard_normal(out[name].shape)
        drawn = base * np.exp(spread * noise) if base else spread * noise
        out[name] = jnp.asarray(drawn.astype(out[name].dtype))
    for name, factor in factors.items():
        out[name] = (out[name] * factor).astype(out[name].dtype)
    return out
```

```python
from contextlib import ExitStack

import numpy as np

import concourse.bass as bass
from concourse import mybir

F32 = mybir.dt.float32
F32R = mybir.dt.float32r
F16 = mybir.dt.float16
BF16 = mybir.dt.bfloat16
U32 = mybir.dt.uint32
ALU = mybir.AluOpType
ACT = mybir.ActivationFunctionType
AX = mybir.AxisListType

P = 128
B, S, D = 8, 512, 256
NT = S // P
DC = D // P
HALVES = 2
LH, LD = 32, 64
LI = LH * LD // HALVES
CH = 4
CW = LI // CH
CP = CW // P
HC = CW // LD
VW = LD + 1
FH, FD = 16, 16
GH = FH // HALVES
HP = GH // 2
PARTS = 3
FV = PARTS * (FD + 1)
E, I = 8, 512
IC = I // P
MASKED = -3.0e38
EPS = 1e-05
R = 5

units = [(i, hp) for i in reversed(range(NT)) for hp in range(HP)]

PRODUCTS = ((0, 0), (0, 1), (1, 0))


AFTER = (5, 10, 13, 19)


def schedule():
    heavy = []
    for c in range(CH):
        before = c - 1
        heavy += [("k", c, 0), ("k", c, 1)]
        if c:
            heavy += [("oT", before, 0), ("oT", before, 1)]
        heavy += [("v", c, 0), ("v", c, 1), ("q", c, 0), ("kv", c), ("q", c, 1)]
        if c:
            heavy += [("y", before, 0), ("y", before, 1)]
        if c == CH - 1:
            heavy += [("xT", 0), ("xT", 1)]
        heavy += [("o", c, t) for t in range(NT)]
    weight = {"k": 4, "v": 4, "q": 4, "kv": 8, "oT": 1.3, "y": 4, "o": 2, "xT": 1.3}
    total = sum(weight[s[0]] for s in heavy)
    first, slack = 28, 2.0
    share = [i + 1 + slack for i, _ in units]
    share += share[-1:] * 3
    scale = (total - first) / sum(share[:len(units) + 1])
    start = [first + scale * sum(share[:n]) for n in range(len(units) + 3)]

    light = []
    for n, (i, hp) in enumerate(units):
        light.append((start[n], ("S", i, hp)))
        light.append((start[n] + AFTER[0], ("E", i, hp)))
        light.append((start[n] + AFTER[1], ("T", i, hp, 0)))
        light.append((start[n] + AFTER[2], ("T", i, hp, 1)))
        light.append((start[n] + AFTER[3], ("AV", i, hp)))
    light += [(14, ("ln0",)), (24, ("ln1",)), (56, ("x2T", 0)), (64, ("x2T", 1))]
    light.sort(key=lambda x: x[0])
    out, at = [("vf",)], 0
    for s in heavy:
        while light and light[0][0] <= at:
            out.append(light.pop(0)[1])
        out.append(s)
        at += weight[s[0]]
    out += [x[1] for x in light]
    out += [("foT",), ("qf",), ("oT", CH - 1, 0), ("oT", CH - 1, 1), ("kf",), ("yf", 0), ("yf", 1),
            ("y", CH - 1, 0), ("y", CH - 1, 1)]
    return out


def wait(eng, semaphore, value, alone=None):
    if alone is not None and not isinstance(value, int):
        register, met = alone
        eng.reg_mov(register, value)
        eng.wait_ge(met, 1)
        value = register
    eng.wait_ge(semaphore, value)


START = [("ln0",), ("ln1",), ("xT", 0), ("xT", 1), ("x2T", 0), ("x2T", 1)]

PRE = [("wf", n) for n in range(4)] + [("W", 0), ("qf",), ("kf",), ("W", 1), ("W", 2), ("W", 3)]


STORED = ("y", CH - 1, 1)
NO_PE = {"W", "ln0", "ln1", "E"}
NO_ACT = {"S", "ln1", "o", "y", "AV", "yf"}
NO_RING = {"S", "AV"}


def takes_part(engine, step):
    if engine == "pe":
        return step[0] not in NO_PE
    if engine == "act":
        return step[0] not in NO_ACT
    if engine == "pool":
        return step in (("ln1",), STORED)
    return step[0] != "E" and (step[0] != "AV" or step[2] == HP - 1)


def attention_phase(nc, x, wq, wk, wv, wo, fwq, fwk, fwv, fwo, w_ln1, linear_out, softmax_out, stack_store):
    BODY = schedule()
    begin = {e: {s: n for n, s in enumerate([s for s in START if takes_part(e, s)])} for e in ("pe", "act", "dve", "pool")}
    first = {e: {s: n for n, s in enumerate([s for s in PRE if takes_part(e, s)])} for e in ("pe", "act", "dve", "pool")}
    index = {e: {s: n for n, s in enumerate([s for s in BODY if takes_part(e, s)])} for e in ("pe", "act", "dve", "pool")}
    nstart = {e: len(begin[e]) for e in begin}
    npre = {e: len(first[e]) for e in first}
    nbody = {e: len(index[e]) for e in index}
    ring_jobs = [s for s in BODY if takes_part("pe", s) and s[0] not in NO_RING]
    ring_bank = {s: n % R for n, s in enumerate(ring_jobs)}
    start_bank = {s: n for n, s in enumerate([s for s in START if takes_part("pe", s)])}
    pre_jobs = [s for s in PRE if takes_part("pe", s)]
    pre_bank = {s: n % R for n, s in enumerate(pre_jobs)}

    with ExitStack() as ctx:
        def sb(name, shape, dt=F32):
            return ctx.enter_context(nc.sbuf_tensor(name, shape, dt))

        def parts(name, shape):
            return [sb(f"{name}_hi", shape, F32R), sb(f"{name}_lo", shape, F32R)]

        def psum(name, shape):
            return ctx.enter_context(nc.psum_tensor(name, shape, F32))

        def sem(name):
            return ctx.enter_context(nc.semaphore(name))

        Wq, Wk, Wv = (parts(f"W{n}", [P, DC, LI]) for n in "qkv")
        Wo = parts("Wo", [P, LI // P, D])
        Fq, Fk, Fv = (parts(f"F{n}", [P, DC, P]) for n in "qkv")
        Fo = parts("Fo", [P, D])
        sc = sb("sc", [P, 2, 2, S])
        o_yl = sb("o_yl", [P, 2, NT, D])
        staged = [sc[:].rearrange("p a b n -> p (a b n)"), o_yl[:].rearrange("p a t n -> p (a t n)")]
        o, yl = o_yl[:, 0], o_yl[:, 1]
        assert CW == D and DC * LI == 4 * S == 2 * NT * D
        staged_f = sb("staged_f", [P, 4, D])
        ident = sb("ident", [P, P])
        mask = sb("mask", [P, S])
        w1 = sb("w1", [P, DC])
        xin = sb("xin", [P, NT, D])
        xn = sb("xn", [P, NT, D])
        xn2 = sb("xn2", [P, NT, D])
        stats = sb("stats", [P, NT, 6])
        moments = sb("moments", [P, NT, 2])
        squares = sb("squares", [P, 2, NT])
        roots = sb("roots", [P, 2, NT])
        scales = sb("scales", [P, 2, NT])
        xT = parts("xT", [P, DC, S])
        x2T = parts("x2T", [P, DC, S])
        k = parts("k", [P, NT, CW])
        v = parts("v", [P, NT, HC, VW])
        kv = parts("kv", [P, CP, 2 * VW])
        q = parts("q", [P, CP, S])
        norm = sb("norm", [P, 2, HC])
        rnorm = sb("rnorm", [P, 2, HC])
        oT = parts("oT", [P, CP, S])
        fqk = [parts("fq", [P, S]), parts("fk", [P, S])]
        qstack = sb("qstack", [P, HP, S], F32R)
        kstack = sb("kstack", [P, HP, S], F32R)
        vrest = sb("vrest", [P, NT, P])
        vf = sb("vf", [P, NT, GH, PARTS, FD + 1], BF16)
        smax = sb("smax", [P, 2, 2])
        sbias = sb("sbias", [P, 2, 2])
        pT = [sb("pT_hi", [P, 2, 2, S], F16), sb("pT_lo", [P, 2, 2, S], F16)]
        fsum = sb("fsum", [P, GH, FD + 1])
        frec = sb("frec", [P, GH])
        fo = sb("fo", [P, NT, GH * FD])
        foT = parts("foT", [P, S])
        yf = sb("yf", [P, NT, D])

        ring = psum("ring", [P, R, 512])
        scores = psum("scores", [P, 2, 512])
        mixed = psum("mixed", [P, 512])

        pe_steps, act_steps, dve_steps, pool_steps = sem("pe_steps"), sem("act_steps"), sem("dve_steps"), sem("pool_steps")
        dve_link = sem("dve_link")
        constants = sem("constants")
        const_in = sem("const_in")
        wf_in = sem("wf_in")
        staged_in = [sem("staged_in0"), sem("staged_in1")]
        first_x_in, x_in = sem("first_x_in"), sem("x_in")
        fqk_stored = sem("fqk_stored")
        stacks_in = sem("stacks_in")
        y_stored = sem("y_stored")
        STACKS, STORES = 16, 16
        progress = {"pe": pe_steps, "act": act_steps, "dve": dve_steps, "pool": pool_steps}

        class Waits:

            def __init__(self, eng, me):
                self.eng, self.me = eng, me
                self.alone = (eng.alloc_register(f"{me}_waited_for"), constants)

            def start(self):
                self.base, self.index, self.seen = dict(nbody), begin, {}

            def half(self, h):
                self.h, self.index = h, first
                self.base = {e: nbody[e] + nstart[e] + h * (npre[e] + B * nbody[e]) for e in progress}
                self.seen = {}

            def batch(self, b):
                self.base = {e: nbody[e] + nstart[e] + npre[e] + self.h * (npre[e] + B * nbody[e]) + b * nbody[e] for e in progress}
                self.index, self.seen = index, {}

            def at(self, e, count, alone=False):
                if self.seen.get(e, -10**9) < count:
                    self.seen[e] = count
                    wait(self.eng, progress[e], self.base[e] + count, self.alone if self.me in ("sp", "pool") or alone else None)

            def on(self, e, step, alone=False):
                self.at(e, self.index[e][step] + 1, alone)

            def last(self, e, step, alone=False):
                if self.index is not begin:
                    self.at(e, index[e][step] + 1 - nbody[e], alone)

            def ended(self, e):
                self.at(e, 0)

        def bank(step, table):
            return ring[:, table[step], :]

        def ring_free(w, step):
            if w.index is begin:
                return
            jobs = pre_jobs if w.index is first else ring_jobs
            n = jobs.index(step)
            if n >= R:
                w.on("dve", jobs[n - R])
            elif w.index is index:
                same = [s for s in jobs if ring_bank[s] == ring_bank[step]]
                w.last("dve", same[-1])

        block = ctx.enter_context(nc.Block())

        @block.gpsimd
        def _(pool):
            pool.memset(ident[:], 0.0).then_inc(constants, 1)
            pool.memset(mask[:], 0.0).then_inc(constants, 1)
            for part, one in zip(v, (1.0, 0.0)):
                pool.memset(part[:].bitcast(F32)[:, :, :, LD:VW], one).then_inc(constants, 1)
            for part in kv:
                pool.memset(part[:].bitcast(F32), 0.0).then_inc(constants, 1)
            pool.memset(vf[:, :, :, :, FD:FD + 1], 0.0).then_inc(constants, 1)
            pool.wait_ge(constants, 7)
            pool.memset(vf[:, :, :, 0, FD:FD + 1], 1.0).then_inc(constants, 1)
            pool.affine_select(out=ident[:], in_=ident[:], compare_op=ALU.not_equal, fill=1.0, base=0,
                               pattern=[[-1, P]], channel_multiplier=1).then_inc(constants, 1)
            pool.affine_select(out=mask[:, S - P:S], in_=mask[:, S - P:S], compare_op=ALU.is_ge, fill=MASKED,
                               base=0, pattern=[[-1, P]], channel_multiplier=1).then_inc(constants, 1)

            w = Waits(pool, "pool")

            def normalised():
                w.on("dve", ("ln1",))
                w.last("pe", ("xT", 1))
                w.last("pe", ("x2T", 1))
                for t in range(NT):
                    for n, out in enumerate((xn, xn2)):
                        last = nc.gpsimd.tensor_scalar(out[:, t, :], xin[:, t, :], moments[:, t, 0:1], scales[:, n, t:t + 1],
                                                       ALU.subtract, ALU.mult)
                last.then_inc(pool_steps, 1)

            def load_x(b):
                pool.dma_start(xin[:], x[b].rearrange("(t p) d -> p t d", p=P)).then_inc(x_in, 16)

            pool.sem_inc(pool_steps, nbody["pool"])
            w.start()
            normalised()
            w.on("pool", ("ln1",))
            load_x(1)
            with pool.Fori(0, HALVES) as h:
                w.half(h)
                cols = [m.rearrange("(c p) (h n) -> h p c n", p=P, h=HALVES)[h] for m in (wq, wk, wv)]
                cols.append(wo.rearrange("(h c p) n -> h p c n", p=P, h=HALVES)[h])
                rows = [m.rearrange("(h p) n -> h p n", h=HALVES)[h] for m in (fwq, fwk, fwv)]
                for n in range(3):
                    pool.dma_start(staged_f[:, n, :], rows[n]).then_inc(wf_in, 16)
                pool.dma_start(staged_f[:, 3, :].rearrange("p (c n) -> p c n", c=DC),
                               fwo.rearrange("(c p) (h n) -> h p c n", p=P, h=HALVES)[h]).then_inc(wf_in, 16)
                w.last("pe", ("T", *units[-1], 1))
                w.last("pool", STORED)
                for n in range(4):
                    if n >= 2:
                        w.on("act", ("W", n - 2))
                        w.on("dve", ("W", n - 2))
                    dst = staged[n % 2].rearrange("p (c n) -> p c n", c=cols[n].shape[1])
                    pool.dma_start(dst, cols[n]).then_inc(staged_in[n % 2], 16)
                with pool.Fori(0, B) as b:
                    w.batch(b)
                    normalised()
                    w.on("pool", ("ln1",))
                    load_x((b + 2) % B)
                    w.on("dve", ("yf", 1))
                    pool.dma_start(softmax_out[h, b].rearrange("(t p) d -> p t d", p=P), yf[:]).then_inc(y_stored, 16)
                    w.on("dve", STORED)
                    pool.dma_start(linear_out[h, b].rearrange("(t p) d -> p t d", p=P), yl).then_inc(y_stored, 16)
                    wait(pool, y_stored, 32 * (h * B + b + 1), w.alone)
                    pool.sem_inc(pool_steps, 1)
            pool.wait_ge(x_in, 16 * (HALVES * B + 1))

        @block.sync
        def _(sp):
            w = Waits(sp, "sp")

            def store_qk(event):
                w.on("act", ("kf",))
                w.on("dve", ("kf",))
                wait(sp, stacks_in, 256 * event + STACKS, w.alone)
                for n in range(2):
                    for a in range(2):
                        sp.dma_start(stack_store[n, a], fqk[n][a][:].bitcast(F32)).then_inc(fqk_stored, 16)
                wait(sp, fqk_stored, 64 * (event + 1) + STORES, w.alone)
                w.on("pe", ("kf",))
                for hh in range(2):
                    for r in range(4):
                        for n, (stack, a) in enumerate(((qstack, r % 2), (kstack, r // 2))):
                            rows = stack_store[n, a].rearrange("(t hh d) s -> hh d t s", hh=2, d=FD)[hh]
                            at = 64 * hh + FD * r
                            sp.dma_start(stack[at:at + FD, :, :].bitcast(F32), rows).then_inc(stacks_in, 16)

            sp.dma_start(xin[:], x[0].rearrange("(t p) d -> p t d", p=P)).then_inc(first_x_in, 16)
            sp.dma_start(w1[:], w_ln1.rearrange("(c p) -> p c", p=P), allow_slow_non_contiguous=True).then_inc(const_in, 16)
            sp.sem_inc(stacks_in, STACKS)
            sp.sem_inc(fqk_stored, STORES)
            sp.wait_ge(constants, 1)
            with sp.Fori(0, HALVES) as h:
                w.half(h)
                store_qk(9 * h)
                with sp.Fori(0, B) as b:
                    w.batch(b)
                    store_qk(9 * h + b + 1)
            sp.wait_ge(stacks_in, 256 * HALVES * (B + 1) + STACKS)

        @block.tensor
        def _(pe):
            w = Waits(pe, "pe")
            pe.wait_ge(constants, 10)

            def products(out, left, right, blocks, start=True, stop=True):
                pairs = [(c, a, b) for c in range(blocks) for a, b in PRODUCTS]
                for n, (c, a, b) in enumerate(pairs):
                    last = nc.tensor.matmul(out, left(a, c), right(b, c), start=start and n == 0,
                                            stop=stop and n == len(pairs) - 1)
                return last

            def step(s, table):
                kind = s[0]
                if kind not in NO_RING:
                    ring_free(w, s)
                    out = bank(s, table)
                if kind == "wf":
                    pe.wait_ge(wf_in, 64 * w.h + 64)
                    for c in range(DC):
                        last = nc.tensor.transpose(out[:, c * P:(c + 1) * P], staged_f[:, s[1], c * P:(c + 1) * P], ident[:])
                elif kind in ("xT", "x2T"):
                    src = xn if kind == "xT" else xn2
                    w.on("pool", ("ln1",))
                    for t in range(NT):
                        last = nc.tensor.transpose(out[:, t * P:(t + 1) * P], src[:, t, s[1] * P:(s[1] + 1) * P], ident[:])
                elif kind in ("qf", "kf"):
                    if table is ring_bank:
                        w.on("dve", ("x2T", 1))
                    if table is pre_bank:
                        w.on("dve", ("wf", 1))
                    weights = Fq if kind == "qf" else Fk
                    last = products(out, lambda a, c: weights[a][:, c, :], lambda b, c: x2T[b][:, c, :], DC)
                elif kind == "vf":
                    w.last("dve", ("x2T", 1))
                    for t in range(NT):
                        last = products(out[:, t * P:(t + 1) * P], lambda a, c: x2T[a][:, c, t * P:(t + 1) * P],
                                        lambda b, c: Fv[b][:, c, :], DC)
                elif kind in ("k", "v"):
                    if s[1] == 0:
                        w.last("dve", ("xT", 1))
                    c0 = s[1] * CW
                    weights = Wk if kind == "k" else Wv
                    for n in range(2):
                        t = 2 * s[2] + n
                        last = products(out[:, n * CW:(n + 1) * CW], lambda a, c: xT[a][:, c, t * P:(t + 1) * P],
                                        lambda b, c: weights[b][:, c, c0:c0 + CW], DC)
                elif kind == "q":
                    c0 = s[1] * CW + s[2] * P
                    last = products(out, lambda a, c: Wq[a][:, c, c0:c0 + P], lambda b, c: xT[b][:, c, :], DC)
                elif kind == "kv":
                    w.on("dve", ("k", s[1], 1))
                    w.on("dve", ("v", s[1], 1))
                    for p in range(CP):
                        last = products(out[:, p * 2 * VW:(p + 1) * 2 * VW], lambda a, t: k[a][:, t, p * P:(p + 1) * P],
                                        lambda b, t: v[b][:, t, 2 * p:2 * p + 2, :], NT)
                elif kind == "o":
                    w.on("dve", ("q", s[1], 1))
                    w.on("dve", ("kv", s[1]))
                    for p in range(CP):
                        last = products(out[:, p * 2 * VW:(p + 1) * 2 * VW], lambda a, _: q[a][:, p, s[2] * P:(s[2] + 1) * P],
                                        lambda b, _: kv[b][:, p, :], 1)
                elif kind == "oT":
                    w.on("dve", ("o", s[1], NT - 1))
                    for t in range(NT):
                        last = nc.tensor.transpose(out[:, t * P:(t + 1) * P], o[:, t, s[2] * P:(s[2] + 1) * P], ident[:])
                elif kind == "y":
                    w.on("dve", ("oT", s[1], 1))
                    for n in range(2):
                        t = 2 * s[2] + n
                        last = products(out[:, n * D:(n + 1) * D], lambda a, p: oT[a][:, p, t * P:(t + 1) * P],
                                        lambda b, p: Wo[b][:, s[1] * CP + p, :], CP)
                elif kind == "S":
                    _, i, hp = s
                    if (i, hp) == (NT - 1, 0):
                        pe.wait_ge(stacks_in, 256 * (w.h * 9 + w.b + 1) + STACKS)
                    n = units.index((i, hp))
                    if n:
                        w.on("dve", ("S", *units[n - 1]))
                    else:
                        w.last("dve", ("S", *units[-1]))
                    for j in range(2):
                        last = nc.tensor.matmul(scores[:, j, 0:(i + 1) * P], qstack[64 * j:64 * j + 64, hp, i * P:(i + 1) * P],
                                                kstack[64 * j:64 * j + 64, hp, 0:(i + 1) * P], start=True, stop=True)
                elif kind == "T":
                    _, i, hp, j = s
                    w.on("act", ("E", i, hp))
                    slot = units.index((i, hp)) % 2
                    for kb in range(i + 1):
                        last = nc.tensor.transpose(out[:, kb * P:(kb + 1) * P], sc[:, slot, j, kb * P:(kb + 1) * P], ident[:])
                elif kind == "AV":
                    _, i, hp = s
                    w.on("dve", ("T", i, hp, 1))
                    w.on("dve", ("vf",))
                    if hp == 0:
                        if i == NT - 1:
                            w.last("dve", ("AV", 0, HP - 1))
                        else:
                            w.on("dve", ("AV", i + 1, HP - 1))
                    slot = units.index((i, hp)) % 2
                    for j in range(2):
                        head = 2 * hp + j
                        for kb in range(i + 1):
                            for a in range(2):
                                last = nc.tensor.matmul(mixed[:, head * FV:(head + 1) * FV], pT[a][:, slot, j, kb * P:(kb + 1) * P],
                                                        vf[:, kb, head, :, :], start=kb == 0 and a == 0, stop=kb == i and a == 1)
                elif kind == "foT":
                    w.on("dve", ("AV", 0, HP - 1))
                    for t in range(NT):
                        last = nc.tensor.transpose(out[:, t * P:(t + 1) * P], fo[:, t, :], ident[:])
                elif kind == "yf":
                    w.on("dve", ("foT",))
                    for n in range(2):
                        t = 2 * s[1] + n
                        last = products(out[:, n * D:(n + 1) * D], lambda a, _: foT[a][:, t * P:(t + 1) * P],
                                        lambda b, _: Fo[b][:], 1)
                last.then_inc(pe_steps, 1)

            pe.sem_inc(pe_steps, nbody["pe"])
            w.start()
            for s in START:
                if takes_part("pe", s):
                    step(s, start_bank)
            with pe.Fori(0, HALVES) as h:
                w.half(h)
                w.ended("dve")
                for s in PRE:
                    if takes_part("pe", s):
                        step(s, pre_bank)
                w.on("dve", PRE[-1], alone=True)
                with pe.Fori(0, B) as b:
                    w.batch(b)
                    w.b = b
                    for s in BODY:
                        if takes_part("pe", s):
                            step(s, ring_bank)

        @block.scalar
        def _(act):
            w = Waits(act, "act")

            def copy(out, in_, func=ACT.Copy, **kw):
                return nc.scalar.activation(out, in_, func, **kw)

            def step(s, table):
                kind = s[0]
                if takes_part("pe", s):
                    w.on("pe", s)
                if kind not in NO_RING and takes_part("pe", s):
                    src = bank(s, table)
                if kind == "W":
                    act.wait_ge(staged_in[s[1] % 2], 32 * w.h + 16 * (s[1] // 2 + 1))
                    dst = (Wq, Wk, Wv, Wo)[s[1]]
                    last = copy(dst[0][:].rearrange("p c n -> p (c n)"), staged[s[1] % 2])
                elif kind == "wf":
                    dst = (Fq, Fk, Fv, Fo)[s[1]][0][:]
                    last = copy(dst, src[:, 0:D] if s[1] == 3 else src[:, 0:D].rearrange("p (c n) -> p c n", c=DC))
                elif kind == "ln0":
                    w.on("dve", s)
                    last = copy(roots[:], squares[:], ACT.Sqrt)
                elif kind == "xT":
                    if table is ring_bank:
                        w.on("pe", ("q", CH - 1, 1))
                    last = copy(xT[0][:, s[1], :], src)
                elif kind == "x2T":
                    last = copy(x2T[0][:, s[1], :], src, scale=w1[:, s[1]:s[1] + 1])
                elif kind in ("qf", "kf"):
                    act.wait_ge(fqk_stored, 64 * w.event + STORES)
                    last = copy(fqk[kind == "kf"][0][:], src)
                elif kind == "vf":
                    w.last("pe", ("AV", 0, HP - 1))
                    last = copy(vf[:, :, :, 0, 0:FD], src.rearrange("p (t h d) -> p t h d", t=NT, h=GH))
                elif kind in ("k", "v"):
                    if s[1]:
                        w.on("pe", ("kv", s[1] - 1))
                    else:
                        w.last("pe", ("kv", CH - 1))
                    if kind == "k":
                        last = copy(k[0][:, 2 * s[2]:2 * s[2] + 2, :], src.rearrange("p (t n) -> p t n", t=2), ACT.Relu)
                    else:
                        last = copy(v[0][:, 2 * s[2]:2 * s[2] + 2, :, 0:LD], src.rearrange("p (t h d) -> p t h d", t=2, h=HC))
                elif kind == "q":
                    if s[1]:
                        w.on("pe", ("o", s[1] - 1, NT - 1))
                    else:
                        w.last("pe", ("o", CH - 1, NT - 1))
                    last = copy(q[0][:, s[2], :], src, ACT.Relu)
                elif kind == "kv":
                    if s[1]:
                        w.on("pe", ("o", s[1] - 1, NT - 1))
                    else:
                        w.last("pe", ("o", CH - 1, NT - 1))
                    pairs = src[:, 0:CP * 2 * VW].rearrange("p (c n) -> p c n", c=CP)
                    copy(kv[0][0:LD, :, 0:VW], pairs[0:LD, :, 0:VW])
                    last = copy(kv[0][LD:P, :, VW:2 * VW], pairs[LD:P, :, VW:2 * VW])
                elif kind == "oT":
                    if s[1]:
                        w.on("pe", ("y", s[1] - 1, 1))
                    else:
                        w.last("pe", ("y", CH - 1, 1))
                    last = copy(oT[0][:, s[2], :], src)
                elif kind == "foT":
                    w.last("pe", ("yf", 1))
                    last = copy(foT[0][:], src)
                elif kind == "E":
                    _, i, hp = s
                    w.on("dve", ("S", i, hp))
                    slot = units.index((i, hp)) % 2
                    for j in range(2):
                        at = sc[:, slot, j, 0:(i + 1) * P]
                        last = copy(at, at, ACT.Exp, bias=sbias[:, slot, j:j + 1], scale=FD ** -0.5)
                elif kind == "T":
                    _, i, hp, j = s
                    n = units.index((i, hp))
                    if n >= 2:
                        w.on("pe", ("AV", *units[n - 2]))
                    else:
                        w.last("pe", ("AV", *units[n - 2]))
                    last = copy(pT[0][:, n % 2, j, 0:(i + 1) * P], src[:, 0:(i + 1) * P])
                last.then_inc(act_steps, 1)

            act.sem_inc(act_steps, nbody["act"])
            act.wait_ge(const_in, 16)
            act.wait_ge(constants, 10)
            w.start()
            for s in START:
                if takes_part("act", s):
                    step(s, start_bank)
            with act.Fori(0, HALVES) as h:
                w.half(h)
                w.event = h * 9
                w.ended("pe")
                for s in PRE:
                    if takes_part("act", s):
                        step(s, pre_bank)
                with act.Fori(0, B) as b:
                    w.batch(b)
                    w.event = h * 9 + b + 1
                    for s in BODY:
                        if takes_part("act", s):
                            step(s, ring_bank)

        @block.vector
        def _(dve):
            w = Waits(dve, "dve")
            linked = [0]

            def link(ins, alone=False):
                linked[0] += 1
                ins.then_inc(dve_link, 1)
                wait(dve, dve_link, w.links + linked[0], w.alone if alone else None)

            def rest(out, src, hi):
                return nc.vector.tensor_tensor(out, src, hi.bitcast(F32), ALU.subtract)

            def step(s, table):
                kind = s[0]
                if takes_part("act", s) and kind not in ("ln0", "S"):
                    w.on("act", s)
                elif takes_part("pe", s):
                    w.on("pe", s, alone=kind == "S")
                if kind not in NO_RING and takes_part("pe", s):
                    src = bank(s, table)
                if kind == "W":
                    dst = (Wq, Wk, Wv, Wo)[s[1]]
                    last = rest(dst[1][:].rearrange("p c n -> p (c n)"), staged[s[1] % 2],
                                dst[0][:].rearrange("p c n -> p (c n)"))
                elif kind == "wf":
                    dst = (Fq, Fk, Fv, Fo)[s[1]]
                    last = rest(dst[1][:], src[:, 0:D] if s[1] == 3 else src[:, 0:D].rearrange("p (c n) -> p c n", c=DC), dst[0][:])
                elif kind == "ln0":
                    if table is start_bank:
                        dve.wait_ge(first_x_in, 16)
                    else:
                        dve.wait_ge(x_in, 16 * w.tokens)
                    w.last("pool", ("ln1",), alone=True)
                    for t in range(NT):
                        ins = nc.vector.bn_stats(stats[:, t, :], xin[:, t, :])
                    link(ins, alone=True)
                    for t in range(NT):
                        ins = nc.vector.bn_aggr(moments[:, t, :], stats[:, t, :])
                    link(ins)
                    link(nc.vector.tensor_scalar(squares[:, 0, :], moments[:, :, 1], EPS, None, ALU.add))
                    last = nc.vector.scalar_tensor_tensor(squares[:, 1, :], squares[:, 0, :], EPS, moments[:, :, 1],
                                                          ALU.mult, ALU.add)
                elif kind == "ln1":
                    w.on("act", ("ln0",))
                    last = nc.vector.reciprocal(scales[:], roots[:])
                elif kind == "xT":
                    last = rest(xT[1][:, s[1], :], src, xT[0][:, s[1], :])
                elif kind == "x2T":
                    last = nc.vector.scalar_tensor_tensor(x2T[1][:, s[1], :], src, w1[:, s[1]:s[1] + 1],
                                                          x2T[0][:, s[1], :].bitcast(F32), ALU.mult, ALU.subtract)
                elif kind in ("qf", "kf"):
                    parts_of = fqk[kind == "kf"]
                    last = rest(parts_of[1][:], src, parts_of[0][:])
                elif kind == "vf":
                    heads = [vf[:, :, :, a, 0:FD] for a in range(PARTS)]
                    rest_h = vrest[:].rearrange("p t (h d) -> p t h d", h=GH)
                    link(nc.vector.tensor_tensor(rest_h, src.rearrange("p (t h d) -> p t h d", t=NT, h=GH), heads[0], ALU.subtract))
                    link(nc.vector.tensor_copy(heads[1], rest_h))
                    last = nc.vector.tensor_tensor(heads[2], rest_h, heads[1], ALU.subtract)
                elif kind == "k":
                    at = slice(2 * s[2], 2 * s[2] + 2)
                    last = nc.vector.scalar_tensor_tensor(k[1][:, at, :], src.rearrange("p (t n) -> p t n", t=2), 0.0,
                                                          k[0][:, at, :].bitcast(F32), ALU.max, ALU.subtract)
                elif kind == "v":
                    at = slice(2 * s[2], 2 * s[2] + 2)
                    last = rest(v[1][:, at, :, 0:LD], src.rearrange("p (t h d) -> p t h d", t=2, h=HC), v[0][:, at, :, 0:LD])
                elif kind == "q":
                    last = nc.vector.scalar_tensor_tensor(q[1][:, s[2], :], src, 0.0, q[0][:, s[2], :].bitcast(F32),
                                                          ALU.max, ALU.subtract)
                elif kind == "kv":
                    pairs = src[:, 0:CP * 2 * VW].rearrange("p (c n) -> p c n", c=CP)
                    rest(kv[1][0:LD, :, 0:VW], pairs[0:LD, :, 0:VW], kv[0][0:LD, :, 0:VW])
                    last = rest(kv[1][LD:P, :, VW:2 * VW], pairs[LD:P, :, VW:2 * VW], kv[0][LD:P, :, VW:2 * VW])
                elif kind == "o":
                    t = s[2]
                    if s[1]:
                        w.on("pe", ("oT", s[1] - 1, 1))
                    else:
                        w.last("pe", ("oT", CH - 1, 1))
                    heads = src[:, 0:HC * VW].rearrange("p (h n) -> p h n", h=HC)
                    link(nc.vector.tensor_scalar(norm[:, t % 2, :], heads[:, :, LD], 1e-06, None, ALU.max))
                    link(nc.vector.reciprocal(rnorm[:, t % 2, :], norm[:, t % 2, :]))
                    last = nc.vector.tensor_tensor(o[:, t, :].rearrange("p (h d) -> p h d", h=HC), heads[:, :, 0:LD],
                                                   rnorm[:, t % 2, :].unsqueeze(2).to_broadcast([P, HC, LD]), ALU.mult)
                elif kind == "oT":
                    last = rest(oT[1][:, s[2], :], src, oT[0][:, s[2], :])
                elif kind == "y":
                    at = yl[:, 2 * s[2]:2 * s[2] + 2, :]
                    new = src.rearrange("p (t n) -> p t n", t=2)
                    if s[1] == 0:
                        w.last("pool", STORED)
                        last = nc.vector.tensor_copy(at, new)
                    else:
                        w.on("dve", ("y", s[1] - 1, s[2]))
                        last = nc.vector.tensor_tensor(at, new, at, ALU.add)
                elif kind == "S":
                    _, i, hp = s
                    n = units.index((i, hp))
                    slot = n % 2
                    if n >= 2:
                        w.on("pe", ("T", *units[n - 2], 1), alone=True)
                    else:
                        w.last("pe", ("T", *units[n - 2], 1), alone=True)
                    for j in range(2):
                        ins = nc.vector.tensor_tensor_reduce(sc[:, slot, j, 0:(i + 1) * P], scores[:, j, 0:(i + 1) * P],
                                                             mask[:, S - (i + 1) * P:S], 1.0, MASKED, ALU.add, ALU.max,
                                                             smax[:, slot, j:j + 1])
                    link(ins)
                    last = nc.vector.tensor_scalar(sbias[:, slot, :], smax[:, slot, :], -FD ** -0.5, None, ALU.mult)
                elif kind == "T":
                    _, i, hp, j = s
                    slot = units.index((i, hp)) % 2
                    last = nc.vector.tensor_tensor(pT[1][:, slot, j, 0:(i + 1) * P], src[:, 0:(i + 1) * P],
                                                   pT[0][:, slot, j, 0:(i + 1) * P], ALU.subtract)
                elif kind == "AV":
                    _, i, _ = s
                    if i == NT - 1:
                        w.last("pe", ("foT",))
                    link(nc.vector.tensor_reduce(fsum[:], mixed[:, 0:GH * FV].rearrange("p (h a d) -> p h d a", h=GH, a=PARTS),
                                                 AX.X, ALU.add))
                    link(nc.vector.reciprocal(frec[:], fsum[:, :, FD]))
                    last = nc.vector.tensor_tensor(fo[:, i, :].rearrange("p (h d) -> p h d", h=GH), fsum[:, :, 0:FD],
                                                   frec[:].unsqueeze(2).to_broadcast([P, GH, FD]), ALU.mult)
                elif kind == "foT":
                    last = rest(foT[1][:], src, foT[0][:])
                elif kind == "yf":
                    if s[1] == 0:
                        w.last("pool", STORED)
                    last = nc.vector.tensor_copy(yf[:, 2 * s[1]:2 * s[1] + 2, :], src.rearrange("p (t n) -> p t n", t=2))
                last.then_inc(dve_steps, 1)

            def links(steps):
                return sum({"ln0": 3, "vf": 2, "o": 2, "S": 1, "AV": 2}.get(s[0], 0)
                           for s in steps if takes_part("dve", s))

            dve.sem_inc(dve_steps, nbody["dve"])
            dve.wait_ge(const_in, 16)
            dve.wait_ge(constants, 10)
            w.start()
            w.tokens, w.links = 0, 0
            for s in START:
                if takes_part("dve", s):
                    step(s, start_bank)
            with dve.Fori(0, HALVES) as h:
                w.half(h)
                w.links, linked[0] = links(START) + h * (links(PRE) + B * links(BODY)), 0
                w.ended("pe")
                for s in PRE:
                    if takes_part("dve", s):
                        step(s, pre_bank)
                assert linked[0] == links(PRE)
                with dve.Fori(0, B) as b:
                    w.batch(b)
                    w.b = b
                    w.tokens = h * B + b + 1
                    w.links, linked[0] = links(START) + h * (links(PRE) + B * links(BODY)) + links(PRE) + b * links(BODY), 0
                    for s in BODY:
                        if takes_part("dve", s):
                            step(s, ring_bank)
                    assert linked[0] == links(BODY)


PREP = [("prep", m, j) for m in "gud" for j in range(2)]
EXPERT = [("cw",), ("g", 0), ("u", 0), ("g", 1), ("u", 1), ("h", 0), ("g", 2), ("u", 2), ("h", 1), ("d", 0),
          ("g", 3), ("u", 3), ("h", 2), ("d", 1), ("h", 3), ("d", 2), ("d", 3)]
ROUTE = [("norm", 0), ("norm", 1), ("norm", 2), ("mT", 0), ("mT", 1), ("logits",), ("tokens",), ("top",), ("weights",)]
BOTH = (EXPERT[:1] + ROUTE[:1] + EXPERT[1:4] + ROUTE[1:2] + EXPERT[4:6] + ROUTE[2:3] + EXPERT[6:8] + ROUTE[3:5] +
        EXPERT[8:11] + ROUTE[5:6] + EXPERT[11:13] + ROUTE[6:8] + EXPERT[13:15] + ROUTE[8:9] + EXPERT[15:])
R3 = 6
PARTS_OF = {"prep": ("pe", "act", "dve"), "cw": ("dve",), "g": ("pe", "act"), "u": ("pe", "dve"), "h": ("act", "dve"),
            "d": ("pe", "dve"), "norm": ("act", "dve"), "mT": ("pe", "act", "dve"), "logits": ("pe", "dve"),
            "tokens": ("pe", "dve"), "top": ("act", "dve"), "weights": ("dve",)}


def takes(e, s):
    if s[0] == "norm" and s[1] == 2:
        return e == "dve"
    if s[0] == "d":
        return e == "pe" or e == "dve" and s[1] == IC - 1
    return e in PARTS_OF[s[0]]


def count(e, steps):
    return sum(takes(e, s) for s in steps)


def expert_phase(nc, x, bo, linear_in, softmax_in, w_ln2, wr, wg, wu, wd, out):
    engines = ("pe", "act", "dve")
    start = {e: count(e, PREP + ROUTE + PREP) for e in engines}
    n_both = {e: count(e, BOTH) for e in engines}
    n_expert = {e: count(e, EXPERT) for e in engines}
    n_prep = {e: count(e, PREP) for e in engines}
    AHEAD = dict(n_both)
    after_first = {e: start[e] + (B - 1) * n_both[e] + n_expert[e] for e in engines}
    one_expert = {e: n_prep[e] + B * n_expert[e] for e in engines}
    index_of = {}
    for name, steps in (("prep", PREP), ("route", ROUTE), ("both", BOTH), ("expert", EXPERT)):
        index_of[name] = {e: {s: n for n, s in enumerate([s for s in steps if takes(e, s)])} for e in engines}

    def expert_start(ex):
        return {e: after_first[e] + ex * one_expert[e] - B * n_expert[e] for e in engines}

    with ExitStack() as ctx:
        def sb(name, shape, dt=F32):
            return ctx.enter_context(nc.sbuf_tensor(name, shape, dt))

        def parts(name, shape):
            return [sb(f"{name}_hi", shape, F32R), sb(f"{name}_lo", shape, F32R)]

        def sem(name):
            return ctx.enter_context(nc.semaphore(name))

        xmT = parts("xmT", [P, DC, B * S])
        acc = sb("acc", [P, B * NT, D])
        WgT = [parts(f"WgT{n}", [P, DC, I]) for n in range(2)]
        WuT = [parts(f"WuT{n}", [P, DC, I]) for n in range(2)]
        WdT = [parts(f"WdT{n}", [P, IC, D]) for n in range(2)]
        raw = {"g": sb("raw_g", [P, IC, D]), "u": sb("raw_u", [P, IC, D]), "d": sb("raw_d", [P, DC, I])}
        WrT = parts("WrT", [P, DC, P])
        raw_r = sb("raw_r", [P, DC, E])
        identity = sb("identity", [P, P])
        w2 = sb("w2", [P, D])
        bias = sb("bias", [P, D])
        silu = sb("silu", [P, 2, S])
        h = sb("h", [P, 2, S])
        hT = parts("hT", [P, IC, S])
        cw = sb("cw", [P, E, B * NT])
        cw_now = sb("cw_now", [P, NT])
        xt = sb("xt", [P, NT, D])
        lin = sb("lin", [P, 2, NT, D])
        sof = sb("sof", [P, 2, NT, D])
        logitsT = lin[:, 1].rearrange("p t d -> p (t d)")[:, 0:S]
        stats = sb("stats3", [P, NT, 6])
        moments = sb("moments3", [P, NT, 2])
        small = sb("small", [P, 10, NT])
        var_eps, std, rstd, ms_eps, rms, rrms, gap, expgap, p0, p1 = (small[:, n, :] for n in range(10))
        logits = sb("logits", [P, NT, E])
        top = sb("top", [P, NT, 8])
        top_at = sb("top_at", [P, NT, 8], U32)
        top_f = sb("top_f", [P, NT, 8])
        experts = sb("experts", [P, NT, E])
        chosen = sb("chosen", [P, 2, NT, E])

        ring = ctx.enter_context(nc.psum_tensor("ring3", [P, R3, 512], F32))
        down = ctx.enter_context(nc.psum_tensor("down", [P, 2, 512], F32))

        progress = {"pe": sem("pe_steps3"), "act": sem("act_steps3"), "dve": sem("dve_steps3")}
        pool_steps = sem("pool_steps3")
        dve_link = sem("dve_link3")
        constants = sem("constants3")
        const_in = sem("const_in3")
        raw_in = sem("raw_in")
        tokens_in = sem("tokens_in")
        stored = sem("stored")

        class Waits:
            def __init__(self, eng, me):
                self.eng = eng
                self.alone = (eng.alloc_register(f"{me}_waited_for3"), constants)

            def enter(self, table, base):
                self.table, self.index, self.base, self.seen = table, index_of[table], base, {}

            def at(self, e, n, alone=False):
                if self.seen.get(e, -10**9) < n:
                    self.seen[e] = n
                    wait(self.eng, progress[e], self.base[e] + AHEAD[e] + n, self.alone if alone else None)

            def on(self, e, step, alone=False):
                self.at(e, self.index[e][step] + 1, alone)

            def last(self, e, step, alone=False):
                self.at(e, self.index[e][step] + 1 - len(self.index[e]), alone)

            def before(self, e):
                self.at(e, 0)

        def ring_jobs(table):
            steps = {"both": BOTH, "expert": EXPERT, "route": ROUTE}[table]
            return [s for s in steps if takes("pe", s) and s[0] != "d"]

        def bank(table, s):
            return ring[:, ring_jobs(table).index(s) % R3, :]

        def freed_by(s):
            return ("u", s[1]) if s[0] == "g" else s

        def ring_free(w, s):
            jobs = ring_jobs(w.table)
            n = jobs.index(s)
            if n >= R3:
                w.on("dve", freed_by(jobs[n - R3]))
            elif w.table != "route":
                w.last("dve", freed_by([j for m, j in enumerate(jobs) if m % R3 == n][-1]))

        def run(w, me, step, fori):
            def steps(table, base, what, **at):
                w.enter(table, base)
                for s in what:
                    if takes(me, s):
                        step(s, w, **at)

            zero = {e: 0 for e in engines}
            steps("prep", zero, PREP, nxt=0, parity=0)
            steps("route", {e: n_prep[e] for e in engines}, ROUTE, to=0)
            steps("prep", {e: n_prep[e] + count(e, ROUTE) for e in engines}, PREP, nxt=1, parity=1)
            with fori(0, B - 1) as n:
                steps("both", {e: start[e] + n * n_both[e] for e in engines}, BOTH, n=n, ex=0, parity=0, to=n + 1)
            steps("expert", {e: after_first[e] - n_expert[e] for e in engines}, EXPERT, n=B - 1, ex=0, parity=0)
            with fori(0, (E - 2) // 2) as pair:
                for k in range(2):
                    ex = 2 * pair + 1 + k
                    base = expert_start(ex)
                    steps("prep", {e: base[e] - n_prep[e] for e in engines}, PREP, nxt=ex + 1, parity=k)
                    with fori(0, B) as n:
                        steps("expert", {e: base[e] + n * n_expert[e] for e in engines}, EXPERT, n=n, ex=ex, parity=1 - k)
            base = {e: expert_start(E - 1)[e] - n_prep[e] for e in engines}
            with fori(0, B) as n:
                steps("expert", {e: base[e] + n * n_expert[e] for e in engines}, EXPERT, n=n, ex=E - 1, parity=1)

        block = ctx.enter_context(nc.Block())

        @block.gpsimd
        def _(pool):
            pool.memset(identity[:], 0.0).then_inc(constants, 1)
            for part in WrT:
                pool.memset(part[:].bitcast(F32), 0.0).then_inc(constants, 1)
            pool.wait_ge(constants, 3)
            pool.affine_select(out=identity[:], in_=identity[:], compare_op=ALU.not_equal, fill=1.0, base=0,
                               pattern=[[-1, P]], channel_multiplier=1).then_inc(constants, 1)
            pool.iota(experts[:], pattern=[[0, NT], [1, E]], base=0, channel_multiplier=0,
                      allow_small_or_imprecise_dtypes=True).then_inc(constants, 1)
            pool.wait_ge(const_in, 64)
            with pool.Fori(0, B) as n:
                pool.wait_ge(tokens_in, 80 * n + 80)
                nc.gpsimd.tensor_tensor(lin[:, 0], lin[:, 0], lin[:, 1], ALU.add).then_inc(pool_steps, 1)
                pool.wait_ge(pool_steps, 3 * n + 1)
                nc.gpsimd.tensor_tensor(lin[:, 0], lin[:, 0], xt[:], ALU.add).then_inc(pool_steps, 1)
                pool.wait_ge(pool_steps, 3 * n + 2)
                nc.gpsimd.tensor_tensor(lin[:, 0], lin[:, 0], bias[:].unsqueeze(1).to_broadcast([P, NT, D]),
                                        ALU.add).then_inc(pool_steps, 1)

        @block.sync
        def _(sp):
            def rows(m):
                return m.rearrange("(t p) d -> p t d", p=P)

            def load_weights(ex):
                sp.dma_start(raw["g"][:], rows(wg[ex])).then_inc(raw_in, 16)
                sp.dma_start(raw["u"][:], rows(wu[ex])).then_inc(raw_in, 16)
                sp.dma_start(raw["d"][:], rows(wd[ex])).then_inc(raw_in, 16)

            def load_tokens(n, table, base):
                def ended(e, step):
                    if table:
                        wait(sp, progress[e], AHEAD[e] + base[e] + index_of[table][e][step] + 1, alone)

                ended("dve", ("norm", 2))
                sp.dma_start(xt[:], rows(x[n])).then_inc(tokens_in, 16)
                sp.dma_start(lin[:, 0], rows(linear_in[0, n])).then_inc(tokens_in, 16)
                for k in range(HALVES):
                    if k:
                        ended("pe", ("mT", 1))
                    sp.dma_start(sof[:, k], rows(softmax_in[k, n])).then_inc(tokens_in, 16)
                ended("pe", ("tokens",))
                sp.dma_start(lin[:, 1], rows(linear_in[1, n])).then_inc(tokens_in, 16)

            sp.wait_ge(constants, 1)
            alone = (sp.alloc_register("sp_waited_for3"), constants)
            load_tokens(0, None, None)
            load_weights(0)
            sp.dma_start(w2[:], w_ln2.partition_broadcast(P)).then_inc(const_in, 16)
            sp.dma_start(bias[:], bo.partition_broadcast(P)).then_inc(const_in, 16)
            for c in range(DC):
                sp.dma_start(raw_r[:, c, :], wr[:, c * P:(c + 1) * P].rearrange("e p -> p e"), allow_slow_non_contiguous=True)\
                    .then_inc(const_in, 16)
            wait(sp, progress["pe"], AHEAD["pe"] + n_prep["pe"], alone)
            load_weights(1)
            load_tokens(1, "route", n_prep)
            wait(sp, progress["pe"], AHEAD["pe"] + start["pe"], alone)
            load_weights(2)
            with sp.Fori(0, B - 2) as n:
                load_tokens(n + 2, "both", {e: start[e] + n * n_both[e] for e in engines})
            with sp.Fori(3, E) as ex:
                wait(sp, progress["pe"], AHEAD["pe"] + after_first["pe"] + (ex - 3) * one_expert["pe"] + n_prep["pe"], alone)
                load_weights(ex)
            with sp.Fori(0, B) as n:
                wait(sp, progress["dve"], AHEAD["dve"] + expert_start(E - 1)["dve"] - n_prep["dve"] + (n + 1) * n_expert["dve"], alone)
                sp.dma_start(rows(out[n]), acc[:, bass.ds(NT * n, NT), :]).then_inc(stored, 16)
            sp.wait_ge(stored, 16 * B)

        @block.tensor
        def _(pe):
            w = Waits(pe, "pe")

            def products(out, left, right, blocks):
                pairs = [(c, a, b) for c in range(blocks) for a, b in PRODUCTS]
                for m, (c, a, b) in enumerate(pairs):
                    last = nc.tensor.matmul(out, left(a, c), right(b, c), start=m == 0, stop=m == len(pairs) - 1)
                return last

            def step(s, w, n=None, ex=None, parity=None, to=None, nxt=None):
                kind = s[0]
                if kind not in ("prep", "d"):
                    ring_free(w, s)
                    dst = bank(w.table, s)
                if kind == "prep":
                    job = PREP.index(s)
                    if job == 0:
                        pe.wait_ge(raw_in, 48 * nxt + 48)
                        w.before("dve")
                    if job >= 2:
                        w.on("dve", PREP[job - 2])
                    dst = down[:, job % 2, :]
                    for m in range(4):
                        if s[1] == "d":
                            src = raw["d"][:, m % 2, (2 * s[2] + m // 2) * P:(2 * s[2] + m // 2 + 1) * P]
                        else:
                            src = raw[s[1]][:, m, s[2] * P:(s[2] + 1) * P]
                        last = nc.tensor.transpose(dst[:, m * P:(m + 1) * P], src, identity[:])
                elif kind in ("g", "u"):
                    weights = (WgT if kind == "g" else WuT)[parity]
                    at = bass.ds(S * n, S)
                    last = products(dst, lambda a, c: weights[a][:, c, s[1] * P:(s[1] + 1) * P],
                                    lambda b, c: xmT[b][:, c, at], DC)
                elif kind == "d":
                    ic = s[1]
                    w.on("dve", ("h", ic))
                    if ic == 0:
                        w.before("dve")
                    for t in range(NT):
                        for m, (a, b) in enumerate(PRODUCTS):
                            last = nc.tensor.matmul(down[:, t // 2, (t % 2) * D:(t % 2 + 1) * D], hT[a][:, ic, t * P:(t + 1) * P],
                                                    WdT[parity][b][:, ic, :], start=ic == 0 and m == 0 and t % 2 == 0,
                                                    stop=ic == IC - 1 and m == 2, skip_group_check=True)
                elif kind == "mT":
                    w.on("dve", ("norm", 2))
                    for t in range(NT):
                        last = nc.tensor.transpose(dst[:, t * P:(t + 1) * P], sof[:, 1, t, s[1] * P:(s[1] + 1) * P], identity[:])
                elif kind == "logits":
                    w.on("dve", ("mT", 1))
                    last = products(dst, lambda a, c: WrT[a][:, c, :], lambda b, c: xmT[b][:, c, bass.ds(S * to, S)], DC)
                elif kind == "tokens":
                    w.on("dve", ("logits",))
                    for t in range(NT):
                        last = nc.tensor.transpose(dst[:, t * P:(t + 1) * P], logitsT[:, t * P:(t + 1) * P], identity[:])
                last.then_inc(progress["pe"], 1)

            pe.sem_inc(progress["pe"], AHEAD["pe"])
            pe.wait_ge(constants, 7)
            run(w, "pe", step, pe.Fori)

        @block.scalar
        def _(act):
            w = Waits(act, "act")

            def copy(out, in_, func=ACT.Copy):
                return nc.scalar.activation(out, in_, func)

            def step(s, w, n=None, ex=None, parity=None, to=None, nxt=None):
                kind = s[0]
                if kind in ("prep", "g", "mT"):
                    w.on("pe", s)
                if kind == "prep":
                    dst = {"g": WgT, "u": WuT, "d": WdT}[s[1]][parity][0]
                    if s[1] == "d":
                        last = copy(dst[:, 2 * s[2]:2 * s[2] + 2, :], down[:, PREP.index(s) % 2, :].rearrange("p (c n) -> p c n", c=2))
                    else:
                        last = copy(dst[:, s[2], :], down[:, PREP.index(s) % 2, :])
                elif kind == "g":
                    if s[1] >= 2:
                        w.on("dve", ("u", s[1] - 2))
                    else:
                        w.last("dve", ("u", s[1] + 2))
                    last = copy(silu[:, s[1] % 2, :], bank(w.table, s), ACT.Silu)
                elif kind == "h":
                    w.on("dve", ("u", s[1]))
                    w.last("pe", ("d", s[1]))
                    last = copy(hT[0][:, s[1], :], h[:, s[1] % 2, :])
                elif kind == "norm":
                    w.on("dve", s)
                    last = copy((std, rms)[s[1]], (var_eps, ms_eps)[s[1]], ACT.Sqrt)
                elif kind == "mT":
                    last = copy(xmT[0][:, s[1], bass.ds(S * to, S)], bank(w.table, s))
                elif kind == "top":
                    w.on("dve", s)
                    last = copy(expgap, gap, ACT.Exp)
                last.then_inc(progress["act"], 1)

            act.sem_inc(progress["act"], AHEAD["act"])
            act.wait_ge(const_in, 64)
            act.wait_ge(constants, 5)
            nc.scalar.activation(WrT[0][:, :, 0:E], raw_r[:], ACT.Copy).then_inc(constants, 1)
            run(w, "act", step, act.Fori)

        @block.vector
        def _(dve):
            w = Waits(dve, "dve")
            linked = [0]
            LINKS = {"norm": {0: 2, 1: 4, 2: 1}, "logits": {None: 0}, "top": {None: 4}, "weights": {None: 6}}

            def links(steps):
                return sum(LINKS[s[0]][s[1] if len(s) > 1 else None] for s in steps if s[0] in LINKS)

            def link(ins, alone=False):
                linked[0] += 1
                ins.then_inc(dve_link, 1)
                wait(dve, dve_link, w.routed * links(ROUTE) + linked[0], w.alone if alone else None)

            def rest(out, src, hi):
                return nc.vector.tensor_tensor(out, src, hi.bitcast(F32), ALU.subtract)

            def step(s, w, n=None, ex=None, parity=None, to=None, nxt=None):
                kind = s[0]
                if to is not None:
                    w.routed = to
                if s == ROUTE[0]:
                    linked[0] = 0
                if kind in ("prep", "mT", "h"):
                    w.on("act", s)
                elif kind in ("u", "d", "logits", "tokens"):
                    w.on("pe", s)
                if kind == "prep":
                    dst = {"g": WgT, "u": WuT, "d": WdT}[s[1]][parity]
                    src = down[:, PREP.index(s) % 2, :]
                    if s[1] == "d":
                        at = slice(2 * s[2], 2 * s[2] + 2)
                        last = rest(dst[1][:, at, :], src.rearrange("p (c n) -> p c n", c=2), dst[0][:, at, :])
                    else:
                        last = rest(dst[1][:, s[2], :], src, dst[0][:, s[2], :])
                elif kind == "cw":
                    w.last("dve", ("d", IC - 1))
                    last = nc.vector.tensor_copy(cw_now[:], cw[:, ex, bass.ds(NT * n, NT)])
                elif kind == "u":
                    w.on("act", ("g", s[1]))
                    if s[1] >= 2:
                        w.on("act", ("h", s[1] - 2))
                        w.on("dve", ("h", s[1] - 2))
                    else:
                        w.last("act", ("h", s[1] + 2))
                        w.last("dve", ("h", s[1] + 2))
                    last = nc.vector.tensor_tensor(h[:, s[1] % 2, :], bank(w.table, s), silu[:, s[1] % 2, :], ALU.mult)
                elif kind == "h":
                    w.last("pe", ("d", s[1]))
                    last = rest(hT[1][:, s[1], :], h[:, s[1] % 2, :], hT[0][:, s[1], :])
                elif kind == "d":
                    w.on("dve", ("cw",))
                    for t in range(NT):
                        at = acc[:, bass.ds(NT * n + t, 1), :].rearrange("p o d -> p (o d)")
                        last = nc.vector.scalar_tensor_tensor(at, down[:, t // 2, (t % 2) * D:(t % 2 + 1) * D], cw_now[:, t:t + 1],
                                                              at, ALU.mult, ALU.add)
                elif s == ("norm", 0):
                    dve.wait_ge(tokens_in, 80 * to + 80)
                    for t in range(NT):
                        ins = nc.vector.bn_stats(stats[:, t, :], xt[:, t, :])
                    link(ins, alone=True)
                    for t in range(NT):
                        ins = nc.vector.bn_aggr(moments[:, t, :], stats[:, t, :])
                    link(ins)
                    last = nc.vector.tensor_scalar(var_eps, moments[:, :, 1], EPS, None, ALU.add)
                elif s == ("norm", 1):
                    w.on("act", ("norm", 0))
                    link(nc.vector.reciprocal(rstd, std))
                    dve.wait_ge(pool_steps, 3 * to + 3)
                    for t in range(NT):
                        ins = nc.vector.tensor_scalar(xt[:, t, :], xt[:, t, :], moments[:, t, 0:1], rstd[:, t:t + 1],
                                                      ALU.subtract, ALU.mult)
                    link(nc.vector.tensor_tensor(sof[:, 0], sof[:, 0], sof[:, 1], ALU.add))
                    link(nc.vector.tensor_tensor(sof[:, 0], sof[:, 0], xt[:], ALU.add))
                    for t in range(NT):
                        last = nc.vector.tensor_tensor_reduce(sof[:, 1, t, :], sof[:, 0, t, :], sof[:, 0, t, :], 1.0 / D, EPS,
                                                              ALU.mult, ALU.add, ms_eps[:, t:t + 1])
                    link(last)
                    last = nc.vector.tensor_tensor(acc[:, bass.ds(NT * to, NT), :], lin[:, 0], sof[:, 0], ALU.add)
                elif s == ("norm", 2):
                    w.on("act", ("norm", 1))
                    link(nc.vector.reciprocal(rrms, rms))
                    for t in range(NT):
                        last = nc.vector.scalar_tensor_tensor(sof[:, 1, t, :], sof[:, 0, t, :], rrms[:, t:t + 1], w2[:],
                                                              ALU.mult, ALU.mult)
                elif kind == "mT":
                    src = bank(w.table, s)
                    last = rest(xmT[1][:, s[1], bass.ds(S * to, S)], src, xmT[0][:, s[1], bass.ds(S * to, S)])
                elif kind == "logits":
                    last = nc.vector.tensor_copy(logitsT, bank(w.table, s))
                elif kind == "tokens":
                    last = nc.vector.tensor_copy(logits[:], bank(w.table, s).rearrange("p (t n) -> p t n", t=NT)[:, :, 0:E])
                elif kind == "top":
                    w.on("dve", ("tokens",), alone=True)
                    for t in range(NT):
                        ins = nc.vector.max(top[:, t, :], logits[:, t, :])
                    link(ins, alone=True)
                    for t in range(NT):
                        ins = nc.vector.max_index(top_at[:, t, :], top[:, t, :], logits[:, t, :])
                    link(ins)
                    link(nc.vector.tensor_copy(top_f[:], top_at[:]))
                    link(nc.vector.tensor_tensor(gap, top[:, :, 1], top[:, :, 0], ALU.subtract))
                    for k in range(2):
                        last = nc.vector.tensor_tensor(chosen[:, k], experts[:], top_f[:, :, k].unsqueeze(2).to_broadcast([P, NT, E]),
                                                       ALU.is_equal)
                elif kind == "weights":
                    w.on("act", ("top",))
                    w.on("dve", ("top",))
                    link(nc.vector.tensor_scalar(p1, expgap, 1.0, None, ALU.add))
                    link(nc.vector.reciprocal(p0, p1))
                    link(nc.vector.tensor_tensor(p1, expgap, p0, ALU.mult))
                    for k, pk in enumerate((p0, p1)):
                        link(nc.vector.tensor_tensor(chosen[:, k], chosen[:, k], pk.unsqueeze(2).to_broadcast([P, NT, E]), ALU.mult))
                    link(nc.vector.tensor_tensor(chosen[:, 0], chosen[:, 0], chosen[:, 1], ALU.add))
                    last = nc.vector.tensor_copy(cw[:, :, bass.ds(NT * to, NT)], chosen[:, 0].rearrange("p t e -> p e t"))
                last.then_inc(progress["dve"], 1)

            dve.sem_inc(progress["dve"], AHEAD["dve"])
            dve.wait_ge(constants, 6)
            rest(WrT[1][:, :, 0:E], raw_r[:], WrT[0][:, :, 0:E]).then_inc(constants, 1)
            run(w, "dve", step, dve.Fori)
            assert linked[0] == links(ROUTE), (linked[0], links(ROUTE))


_INS = ["L0_attn_hidden_states", "L0_attn_Wq", "L0_attn_Wk", "L0_attn_Wv", "L0_attn_Wo", "L0_attn_bo",
        "L0_ffn_Wq", "L0_ffn_Wk", "L0_ffn_Wv", "L0_ffn_Wo", "L0_ffn_w_ln1", "L0_ffn_w_ln2",
        "L0_ffn_Wr", "L0_ffn_Wg", "L0_ffn_Wu", "L0_ffn_Wd"]


def program(nc, x, wq, wk, wv, wo, bo, fwq, fwk, fwv, fwo, w_ln1, w_ln2, wr, wg, wu, wd, out):
    linear_parts = nc.dram_tensor("linear_parts", [HALVES, B, S, D], F32, kind="Internal").ap()
    softmax_parts = nc.dram_tensor("softmax_parts", [HALVES, B, S, D], F32, kind="Internal").ap()
    stack_store = nc.dram_tensor("stack_store", [2, 2, P, S], F32, kind="Internal").ap()
    attention_phase(nc, x, wq, wk, wv, wo, fwq, fwk, fwv, fwo, w_ln1, linear_parts, softmax_parts, stack_store)
    expert_phase(nc, x, bo, linear_parts, softmax_parts, w_ln2, wr, wg, wu, wd, out)


def kernel(**inputs):
    import concourse.bacc as bacc
    from concourse.bass_utils import run_bass_kernel_spmd

    nc = bacc.Bacc("TRN2", target_bir_lowering=False, num_devices=1)
    arrays, args = {}, []
    for name in _INS:
        array = np.ascontiguousarray(inputs[name])
        arrays[f"in_{name}"] = array
        args.append(nc.dram_tensor(f"in_{name}", array.shape, mybir.dt.from_np(array.dtype), kind="ExternalInput").ap())
    out = nc.dram_tensor("out", [B, S, D], F32, kind="ExternalOutput").ap()
    program(nc, *args, out)
    result = run_bass_kernel_spmd(nc, [arrays], core_ids=[0])
    return result.results[0]["out"]
```

```python
from contextlib import ExitStack

import numpy as np

import concourse.bass as bass
from concourse import mybir

F32 = mybir.dt.float32
F32R = mybir.dt.float32r
F16 = mybir.dt.float16
BF16 = mybir.dt.bfloat16
U32 = mybir.dt.uint32
ALU = mybir.AluOpType
ACT = mybir.ActivationFunctionType
AX = mybir.AxisListType

P = 128
B, S, D = 8, 512, 256
NT = S // P
DC = D // P
HALVES = 2
LH, LD = 32, 64
LI = LH * LD // HALVES
CH = 4
CW = LI // CH
CP = CW // P
HC = CW // LD
VW = LD + 1
FH, FD = 16, 16
GH = FH // HALVES
HP = GH // 2
PARTS = 3
FV = PARTS * (FD + 1)
E, I = 8, 512
IC = I // P
MASKED = -3.0e38
EPS = 1e-05
R = 5

units = [(i, hp) for i in reversed(range(NT)) for hp in range(HP)]

PRODUCTS = ((0, 0), (0, 1), (1, 0))


CHUNK = "k0 k1 v0 v1 a0 a1 kv q0 kh q1 y0 o y1"
WEIGHT = {"k": 4, "v": 4, "q": 4, "kv": 3, "kh": 0, "oT": 1.3, "y": 4, "o": 2, "xT": 1.3}
FIRST, SLACK, AFTER = 29, 2.5, (4, 10, 10, 18)
NORM, X2T, QF, END = (14, 24), (58, 66), (172, 180), -1


def schedule():
    heavy = []
    for c in range(CH):
        for s in CHUNK.split():
            if s[0] in "ay":
                heavy += [("oT" if s[0] == "a" else "y", c - 1, int(s[1]))] if c else []
            elif s == "kv":
                heavy += [("kv", c, p) for p in range(CP)]
            elif s == "kh":
                heavy += [("kh", c)]
            elif s == "o":
                if c == CH - 1:
                    heavy += [("xT", 0), ("xT", 1)]
                heavy += [("o", c, t) for t in range(NT)]
            else:
                heavy += [(s[0], c, int(s[1]))]
    total = sum(WEIGHT[s[0]] for s in heavy) + END
    share = [i + 1 + SLACK for i, _ in units]
    scale = (total - FIRST) / sum(share)
    light = [(NORM[0], ("ln0",)), (NORM[1], ("ln1",)), (X2T[0], ("x2T", 0)), (X2T[1], ("x2T", 1)),
             (QF[0], ("qf",)), (QF[1], ("kf",))]
    for n, (i, hp) in enumerate(units):
        start = FIRST + scale * sum(share[:n])
        light.append((start, ("S", i, hp)))
        light.append((start + AFTER[0], ("E", i, hp)))
        light.append((start + AFTER[1], ("T", i, hp, 0)))
        light.append((start + AFTER[2], ("T", i, hp, 1)))
        light.append((start + AFTER[3], ("AV", i, hp)))
    light.sort(key=lambda x: x[0])
    keys, last = ((next(x for x in light if x[1] == s)) for s in (("kf",), ("S", *units[-1])))
    if keys[0] <= last[0]:
        light.remove(keys)
        light.insert(light.index(last) + 1, (last[0], keys[1]))
    out, at = [], 0
    for s in heavy:
        while light and light[0][0] <= at:
            out.append(light.pop(0)[1])
        out.append(s)
        at += WEIGHT[s[0]]
    out += [x[1] for x in light]
    out += [("oT", CH - 1, 0), ("oT", CH - 1, 1), ("foT",), ("vf",), ("yf", 0), ("yf", 1),
            ("y", CH - 1, 0), ("y", CH - 1, 1)]
    return out


def wait(eng, semaphore, value, alone=None):
    if alone is not None and not isinstance(value, int):
        register, met = alone
        eng.reg_mov(register, value)
        eng.wait_ge(met, 1)
        value = register
    eng.wait_ge(semaphore, value)


START = [("ln0",), ("ln1",), ("xT", 0), ("xT", 1), ("x2T", 0), ("x2T", 1)]

PRE = [("wf", n) for n in range(4)] + [("W", 0), ("qf",), ("kf",), ("W", 1), ("vf",), ("W", 2), ("W", 3)]


STORED = ("y", CH - 1, 1)
NO_PE = {"W", "ln0", "ln1", "E", "kh"}
NO_ACT = {"S", "ln1", "o", "y", "AV", "yf"}
NO_RING = {"S", "AV"}


def takes_part(engine, step):
    if engine == "pe":
        return step[0] not in NO_PE
    if engine == "act":
        return step[0] not in NO_ACT
    if engine == "pool":
        return step in (("ln1",), STORED)
    return step[0] != "E" and (step[0] != "AV" or step[2] == HP - 1)


def attention_phase(nc, x, wq, wk, wv, wo, fwq, fwk, fwv, fwo, w_ln1, linear_out, softmax_out, stack_store):
    BODY = schedule()
    begin = {e: {s: n for n, s in enumerate([s for s in START if takes_part(e, s)])} for e in ("pe", "act", "dve", "pool")}
    first = {e: {s: n for n, s in enumerate([s for s in PRE if takes_part(e, s)])} for e in ("pe", "act", "dve", "pool")}
    index = {e: {s: n for n, s in enumerate([s for s in BODY if takes_part(e, s)])} for e in ("pe", "act", "dve", "pool")}
    nstart = {e: len(begin[e]) for e in begin}
    npre = {e: len(first[e]) for e in first}
    nbody = {e: len(index[e]) for e in index}
    ring_jobs = [s for s in BODY if takes_part("pe", s) and s[0] not in NO_RING]
    ring_bank = {s: n % R for n, s in enumerate(ring_jobs)}
    start_bank = {s: n for n, s in enumerate([s for s in START if takes_part("pe", s)])}
    pre_jobs = [s for s in PRE if takes_part("pe", s)]
    pre_bank = {s: n % R for n, s in enumerate(pre_jobs)}

    with ExitStack() as ctx:
        def sb(name, shape, dt=F32):
            return ctx.enter_context(nc.sbuf_tensor(name, shape, dt))

        def parts(name, shape):
            return [sb(f"{name}_hi", shape, F32R), sb(f"{name}_lo", shape, F32R)]

        def psum(name, shape):
            return ctx.enter_context(nc.psum_tensor(name, shape, F32))

        def sem(name):
            return ctx.enter_context(nc.semaphore(name))

        Wq, Wk, Wv = (parts(f"W{n}", [P, DC, LI]) for n in "qkv")
        Wo = parts("Wo", [P, LI // P, D])
        Fq, Fk, Fv = (parts(f"F{n}", [P, DC, P]) for n in "qkv")
        Fo = parts("Fo", [P, D])
        sc = sb("sc", [P, 2, 2, S])
        o_yl = sb("o_yl", [P, 2, NT, D])
        staged = [sc[:].rearrange("p a b n -> p (a b n)"), o_yl[:].rearrange("p a t n -> p (a t n)")]
        o, yl = o_yl[:, 0], o_yl[:, 1]
        assert CW == D and DC * LI == 4 * S == 2 * NT * D
        staged_f = sb("staged_f", [P, 4, D])
        ident = sb("ident", [P, P])
        mask = sb("mask", [P, S])
        w1 = sb("w1", [P, DC])
        xin = sb("xin", [P, NT, D])
        xn = sb("xn", [P, NT, D])
        xn2 = sb("xn2", [P, NT, D])
        stats = sb("stats", [P, NT, 6])
        moments = sb("moments", [P, NT, 2])
        squares = sb("squares", [P, 2, NT])
        roots = sb("roots", [P, 2, NT])
        scales = sb("scales", [P, 2, NT])
        xT = parts("xT", [P, DC, S])
        x2T = parts("x2T", [P, DC, S])
        k = parts("k", [P, NT, CW])
        v_both = sb("v", [P, NT, 2, HC, VW], F32R)
        v = [v_both[:, :, a] for a in range(2)]
        kv_rest = sb("kv_rest", [P, CP, 2 * VW])
        kv_sum = sb("kv_sum", [P, CP, 2 * VW])
        kv = parts("kv", [P, CP, 2 * VW])
        q = parts("q", [P, CP, S])
        norm = sb("norm", [P, 2, HC])
        rnorm = sb("rnorm", [P, 2, HC])
        oT = parts("oT", [P, CP, S])
        fqk = [parts("fq", [P, S]), parts("fk", [P, S])]
        qstack = sb("qstack", [P, HP, S], F32R)
        kstack = sb("kstack", [P, HP, S], F32R)
        vrest = sb("vrest", [P, NT, P])
        vf = sb("vf", [P, NT, GH, PARTS, FD + 1], BF16)
        smax = sb("smax", [P, 2, 2])
        sbias = sb("sbias", [P, 2, 2])
        pT = [sb("pT_hi", [P, 2, 2, S], F16), sb("pT_lo", [P, 2, 2, S], F16)]
        fsum = sb("fsum", [P, GH, FD + 1])
        frec = sb("frec", [P, GH])
        fo = sb("fo", [P, NT, GH * FD])
        foT = parts("foT", [P, S])
        yf = sb("yf", [P, NT, D])

        ring = psum("ring", [P, R, 512])
        scores = psum("scores", [P, 2, 512])
        mixed = psum("mixed", [P, 512])

        pe_steps, act_steps, dve_steps, pool_steps = sem("pe_steps"), sem("act_steps"), sem("dve_steps"), sem("pool_steps")
        dve_link = sem("dve_link")
        constants = sem("constants")
        const_in = sem("const_in")
        wf_in = sem("wf_in")
        staged_in = [sem("staged_in0"), sem("staged_in1")]
        first_x_in, x_in = sem("first_x_in"), sem("x_in")
        fqk_stored = sem("fqk_stored")
        stacks_in = sem("stacks_in")
        y_stored = sem("y_stored")
        STACKS, STORES = 16, 16
        progress = {"pe": pe_steps, "act": act_steps, "dve": dve_steps, "pool": pool_steps}

        class Waits:

            def __init__(self, eng, me):
                self.eng, self.me = eng, me
                self.alone = (eng.alloc_register(f"{me}_waited_for"), constants)

            def start(self):
                self.base, self.index, self.seen = dict(nbody), begin, {}

            def half(self, h):
                self.h, self.index = h, first
                self.base = {e: nbody[e] + nstart[e] + h * (npre[e] + B * nbody[e]) for e in progress}
                self.seen = {}

            def batch(self, b):
                self.base = {e: nbody[e] + nstart[e] + npre[e] + self.h * (npre[e] + B * nbody[e]) + b * nbody[e] for e in progress}
                self.index, self.seen = index, {}

            def at(self, e, count, alone=False):
                if self.seen.get(e, -10**9) < count:
                    self.seen[e] = count
                    wait(self.eng, progress[e], self.base[e] + count, self.alone if self.me in ("sp", "pool") or alone else None)

            def on(self, e, step, alone=False):
                self.at(e, self.index[e][step] + 1, alone)

            def last(self, e, step, alone=False):
                if self.index is not begin:
                    self.at(e, index[e][step] + 1 - nbody[e], alone)

            def ended(self, e):
                self.at(e, 0)

        def bank(step, table):
            return ring[:, table[step], :]

        def ring_free(w, step):
            if w.index is begin:
                return
            jobs = pre_jobs if w.index is first else ring_jobs
            n = jobs.index(step)
            if n >= R:
                w.on("dve", jobs[n - R])
            elif w.index is index:
                same = [s for s in jobs if ring_bank[s] == ring_bank[step]]
                w.last("dve", same[-1])

        block = ctx.enter_context(nc.Block())

        @block.gpsimd
        def _(pool):
            pool.memset(ident[:], 0.0).then_inc(constants, 1)
            pool.memset(mask[:], 0.0).then_inc(constants, 1)
            for part, one in zip(v, (1.0, 0.0)):
                pool.memset(part.bitcast(F32)[:, :, :, LD:VW], one).then_inc(constants, 1)
            pool.memset(kv_sum[:], 0.0).then_inc(constants, 1)
            pool.memset(vf[:, :, :, :, FD:FD + 1], 0.0).then_inc(constants, 1)
            pool.wait_ge(constants, 6)
            pool.memset(vf[:, :, :, 0, FD:FD + 1], 1.0).then_inc(constants, 1)
            pool.affine_select(out=ident[:], in_=ident[:], compare_op=ALU.not_equal, fill=1.0, base=0,
                               pattern=[[-1, P]], channel_multiplier=1).then_inc(constants, 1)
            pool.affine_select(out=mask[:, S - P:S], in_=mask[:, S - P:S], compare_op=ALU.is_ge, fill=MASKED,
                               base=0, pattern=[[-1, P]], channel_multiplier=1).then_inc(constants, 1)

            w = Waits(pool, "pool")

            def normalised():
                w.on("dve", ("ln1",))
                w.last("pe", ("xT", 1))
                w.last("pe", ("x2T", 1))
                for t in range(NT):
                    for n, out in enumerate((xn, xn2)):
                        last = nc.gpsimd.tensor_scalar(out[:, t, :], xin[:, t, :], moments[:, t, 0:1], scales[:, n, t:t + 1],
                                                       ALU.subtract, ALU.mult)
                last.then_inc(pool_steps, 1)

            def load_x(b):
                pool.dma_start(xin[:], x[b].rearrange("(t p) d -> p t d", p=P)).then_inc(x_in, 16)

            pool.sem_inc(pool_steps, nbody["pool"] + nstart["pool"])
            w.start()
            w.on("dve", ("ln1",))
            load_x(1)
            with pool.Fori(0, HALVES) as h:
                w.half(h)
                with pool.Fori(0, B) as b:
                    w.batch(b)
                    normalised()
                    w.on("pool", ("ln1",))
                    load_x((b + 2) % B)
                    w.on("dve", ("yf", 1))
                    pool.dma_start(softmax_out[h, b].rearrange("(t p) d -> p t d", p=P), yf[:]).then_inc(y_stored, 16)
                    w.on("dve", STORED)
                    pool.dma_start(linear_out[h, b].rearrange("(t p) d -> p t d", p=P), yl).then_inc(y_stored, 16)
                    wait(pool, y_stored, 32 * (h * B + b + 1), w.alone)
                    pool.sem_inc(pool_steps, 1)
            pool.wait_ge(x_in, 16 * (HALVES * B + 1))

        @block.sync
        def _(sp):
            w = Waits(sp, "sp")

            def store_qk(event):
                w.on("act", ("kf",))
                w.on("dve", ("kf",))
                wait(sp, stacks_in, 256 * event + STACKS, w.alone)
                for n in range(2):
                    for a in range(2):
                        sp.dma_start(stack_store[n, a], fqk[n][a][:].bitcast(F32)).then_inc(fqk_stored, 16)
                wait(sp, fqk_stored, 64 * (event + 1) + STORES, w.alone)
                w.on("pe", ("kf",))
                for hh in range(2):
                    for r in range(4):
                        for n, (stack, a) in enumerate(((qstack, r % 2), (kstack, r // 2))):
                            rows = stack_store[n, a].rearrange("(t hh d) s -> hh d t s", hh=2, d=FD)[hh]
                            at = 64 * hh + FD * r
                            sp.dma_start(stack[at:at + FD, :, :].bitcast(F32), rows).then_inc(stacks_in, 16)

            sp.dma_start(xin[:], x[0].rearrange("(t p) d -> p t d", p=P)).then_inc(first_x_in, 16)
            sp.dma_start(w1[:], w_ln1.rearrange("(c p) -> p c", p=P), allow_slow_non_contiguous=True).then_inc(const_in, 16)
            sp.sem_inc(stacks_in, STACKS)
            sp.sem_inc(fqk_stored, STORES)
            sp.wait_ge(constants, 1)
            with sp.Fori(0, HALVES) as h:
                w.half(h)
                cols = [m.rearrange("(c p) (h n) -> h p c n", p=P, h=HALVES)[h] for m in (wq, wk, wv)]
                cols.append(wo.rearrange("(h c p) n -> h p c n", p=P, h=HALVES)[h])
                rows = [m.rearrange("(h p) n -> h p n", h=HALVES)[h] for m in (fwq, fwk, fwv)]
                for n in range(3):
                    sp.dma_start(staged_f[:, n, :], rows[n]).then_inc(wf_in, 16)
                sp.dma_start(staged_f[:, 3, :].rearrange("p (c n) -> p c n", c=DC),
                               fwo.rearrange("(c p) (h n) -> h p c n", p=P, h=HALVES)[h]).then_inc(wf_in, 16)
                w.last("pe", ("T", *units[-1], 1))
                w.last("pool", STORED)
                for n in range(4):
                    if n >= 2:
                        w.on("act", ("W", n - 2))
                        w.on("dve", ("W", n - 2))
                    dst = staged[n % 2].rearrange("p (c n) -> p c n", c=cols[n].shape[1])
                    sp.dma_start(dst, cols[n]).then_inc(staged_in[n % 2], 16)
                store_qk(h * (B + 1))
                with sp.Fori(0, B) as b:
                    w.batch(b)
                    store_qk(h * (B + 1) + b + 1)
            sp.wait_ge(stacks_in, 256 * HALVES * (B + 1) + STACKS)

        @block.tensor
        def _(pe):
            w = Waits(pe, "pe")
            pe.wait_ge(constants, 9)

            def products(out, left, right, blocks, start=True, stop=True):
                pairs = [(c, a, b) for c in range(blocks) for a, b in PRODUCTS]
                for n, (c, a, b) in enumerate(pairs):
                    last = nc.tensor.matmul(out, left(a, c), right(b, c), start=start and n == 0,
                                            stop=stop and n == len(pairs) - 1)
                return last

            def step(s, table):
                kind = s[0]
                if kind not in NO_RING:
                    ring_free(w, s)
                    out = bank(s, table)
                if kind == "wf":
                    pe.wait_ge(wf_in, 64 * w.h + 64)
                    for c in range(DC):
                        last = nc.tensor.transpose(out[:, c * P:(c + 1) * P], staged_f[:, s[1], c * P:(c + 1) * P], ident[:])
                elif kind in ("xT", "x2T"):
                    src = xn if kind == "xT" else xn2
                    w.on("dve" if table is start_bank else "pool", ("ln1",))
                    for t in range(NT):
                        last = nc.tensor.transpose(out[:, t * P:(t + 1) * P], src[:, t, s[1] * P:(s[1] + 1) * P], ident[:])
                elif kind in ("qf", "kf"):
                    w.on("dve", ("x2T", 1) if table is ring_bank else ("wf", 1))
                    weights = Fq if kind == "qf" else Fk
                    last = products(out, lambda a, c: weights[a][:, c, :], lambda b, c: x2T[b][:, c, :], DC)
                elif kind == "vf":
                    w.on("dve", ("x2T", 1) if table is ring_bank else ("wf", 2))
                    for t in range(NT):
                        last = products(out[:, t * P:(t + 1) * P], lambda a, c: x2T[a][:, c, t * P:(t + 1) * P],
                                        lambda b, c: Fv[b][:, c, :], DC)
                elif kind in ("k", "v"):
                    if s[1] == 0:
                        w.last("dve", ("xT", 1))
                    c0 = s[1] * CW
                    weights = Wk if kind == "k" else Wv
                    for n in range(2):
                        t = 2 * s[2] + n
                        last = products(out[:, n * CW:(n + 1) * CW], lambda a, c: xT[a][:, c, t * P:(t + 1) * P],
                                        lambda b, c: weights[b][:, c, c0:c0 + CW], DC)
                elif kind == "q":
                    c0 = s[1] * CW + s[2] * P
                    last = products(out, lambda a, c: Wq[a][:, c, c0:c0 + P], lambda b, c: xT[b][:, c, :], DC)
                elif kind == "kv":
                    w.on("dve", ("k", s[1], 1))
                    w.on("dve", ("v", s[1], 1))
                    p = s[2]
                    heads = slice(2 * p, 2 * p + 2)
                    for t in range(NT):
                        for a in ((0, 1) if t < NT - 1 else (1, 0)):
                            left = k[a][:, t, p * P:(p + 1) * P]
                            if a == 0:
                                last = nc.tensor.matmul(out[:, 0:4 * VW], left, v_both[:, t, :, heads, :],
                                                        start=t == 0, stop=t == NT - 1)
                            else:
                                last = nc.tensor.matmul(out[:, 0:2 * VW], left, v_both[:, t, 0, heads, :],
                                                        start=False, stop=False)
                elif kind == "o":
                    w.on("dve", ("q", s[1], 1))
                    w.on("dve", ("kh", s[1]))
                    for p in range(CP):
                        last = products(out[:, p * 2 * VW:(p + 1) * 2 * VW], lambda a, _: q[a][:, p, s[2] * P:(s[2] + 1) * P],
                                        lambda b, _: kv[b][:, p, :], 1)
                elif kind == "oT":
                    w.on("dve", ("o", s[1], NT - 1))
                    for t in range(NT):
                        last = nc.tensor.transpose(out[:, t * P:(t + 1) * P], o[:, t, s[2] * P:(s[2] + 1) * P], ident[:])
                elif kind == "y":
                    w.on("dve", ("oT", s[1], 1))
                    for n in range(2):
                        t = 2 * s[2] + n
                        last = products(out[:, n * D:(n + 1) * D], lambda a, p: oT[a][:, p, t * P:(t + 1) * P],
                                        lambda b, p: Wo[b][:, s[1] * CP + p, :], CP)
                elif kind == "S":
                    _, i, hp = s
                    if (i, hp) == (NT - 1, 0):
                        pe.wait_ge(stacks_in, 256 * (w.h * (B + 1) + w.b + 1) + STACKS)
                    n = units.index((i, hp))
                    if n:
                        w.on("dve", ("S", *units[n - 1]))
                    else:
                        w.last("dve", ("S", *units[-1]))
                    for j in range(2):
                        last = nc.tensor.matmul(scores[:, j, 0:(i + 1) * P], qstack[64 * j:64 * j + 64, hp, i * P:(i + 1) * P],
                                                kstack[64 * j:64 * j + 64, hp, 0:(i + 1) * P], start=True, stop=True)
                elif kind == "T":
                    _, i, hp, j = s
                    w.on("act", ("E", i, hp))
                    slot = units.index((i, hp)) % 2
                    for kb in range(i + 1):
                        last = nc.tensor.transpose(out[:, kb * P:(kb + 1) * P], sc[:, slot, j, kb * P:(kb + 1) * P], ident[:])
                elif kind == "AV":
                    _, i, hp = s
                    w.on("dve", ("T", i, hp, 1))
                    w.last("dve", ("vf",))
                    if hp == 0:
                        if i == NT - 1:
                            w.last("dve", ("AV", 0, HP - 1))
                        else:
                            w.on("dve", ("AV", i + 1, HP - 1))
                    slot = units.index((i, hp)) % 2
                    for j in range(2):
                        head = 2 * hp + j
                        for kb in range(i + 1):
                            for a in range(2):
                                last = nc.tensor.matmul(mixed[:, head * FV:(head + 1) * FV], pT[a][:, slot, j, kb * P:(kb + 1) * P],
                                                        vf[:, kb, head, :, :], start=kb == 0 and a == 0, stop=kb == i and a == 1)
                elif kind == "foT":
                    w.on("dve", ("AV", 0, HP - 1))
                    for t in range(NT):
                        last = nc.tensor.transpose(out[:, t * P:(t + 1) * P], fo[:, t, :], ident[:])
                elif kind == "yf":
                    w.on("dve", ("foT",))
                    for n in range(2):
                        t = 2 * s[1] + n
                        last = products(out[:, n * D:(n + 1) * D], lambda a, _: foT[a][:, t * P:(t + 1) * P],
                                        lambda b, _: Fo[b][:], 1)
                last.then_inc(pe_steps, 1)

            pe.sem_inc(pe_steps, nbody["pe"])
            w.start()
            for s in START:
                if takes_part("pe", s):
                    step(s, start_bank)
            with pe.Fori(0, HALVES) as h:
                w.half(h)
                w.ended("dve")
                for s in PRE:
                    if takes_part("pe", s):
                        step(s, pre_bank)
                w.on("dve", PRE[-1], alone=True)
                with pe.Fori(0, B) as b:
                    w.batch(b)
                    w.b = b
                    for s in BODY:
                        if takes_part("pe", s):
                            step(s, ring_bank)

        @block.scalar
        def _(act):
            w = Waits(act, "act")

            def copy(out, in_, func=ACT.Copy, **kw):
                return nc.scalar.activation(out, in_, func, **kw)

            def step(s, table):
                kind = s[0]
                if takes_part("pe", s):
                    w.on("pe", s)
                if kind not in NO_RING and takes_part("pe", s):
                    src = bank(s, table)
                if kind == "W":
                    act.wait_ge(staged_in[s[1] % 2], 32 * w.h + 16 * (s[1] // 2 + 1))
                    dst = (Wq, Wk, Wv, Wo)[s[1]]
                    last = copy(dst[0][:].rearrange("p c n -> p (c n)"), staged[s[1] % 2])
                elif kind == "wf":
                    dst = (Fq, Fk, Fv, Fo)[s[1]][0][:]
                    last = copy(dst, src[:, 0:D] if s[1] == 3 else src[:, 0:D].rearrange("p (c n) -> p c n", c=DC))
                elif kind == "ln0":
                    w.on("dve", s)
                    last = copy(roots[:], squares[:], ACT.Sqrt)
                elif kind == "xT":
                    if table is ring_bank:
                        w.on("pe", ("q", CH - 1, 1))
                    last = copy(xT[0][:, s[1], :], src)
                elif kind == "x2T":
                    last = copy(x2T[0][:, s[1], :], src, scale=w1[:, s[1]:s[1] + 1])
                elif kind in ("qf", "kf"):
                    act.wait_ge(fqk_stored, 64 * w.event + STORES)
                    last = copy(fqk[kind == "kf"][0][:], src)
                elif kind == "vf":
                    if table is ring_bank:
                        w.on("pe", ("AV", 0, HP - 1))
                    last = copy(vf[:, :, :, 0, 0:FD], src.rearrange("p (t h d) -> p t h d", t=NT, h=GH))
                elif kind in ("k", "v"):
                    if s[1]:
                        w.on("pe", ("kv", s[1] - 1, CP - 1))
                    else:
                        w.last("pe", ("kv", CH - 1, CP - 1))
                    if kind == "k":
                        last = copy(k[0][:, 2 * s[2]:2 * s[2] + 2, :], src.rearrange("p (t n) -> p t n", t=2), ACT.Relu)
                    else:
                        last = copy(v[0][:, 2 * s[2]:2 * s[2] + 2, :, 0:LD], src.rearrange("p (t h d) -> p t h d", t=2, h=HC))
                elif kind == "q":
                    if s[1]:
                        w.on("pe", ("o", s[1] - 1, NT - 1))
                    else:
                        w.last("pe", ("o", CH - 1, NT - 1))
                    last = copy(q[0][:, s[2], :], src, ACT.Relu)
                elif kind == "kv":
                    if s[1]:
                        w.on("dve", ("kv", s[1] - 1, s[2]))
                    else:
                        w.last("dve", ("kv", CH - 1, s[2]))
                    last = copy(kv_rest[:, s[2], :], src[:, 2 * VW:4 * VW])
                elif kind == "kh":
                    w.on("dve", ("kv", s[1], CP - 1))
                    if s[1]:
                        w.on("pe", ("o", s[1] - 1, NT - 1))
                    else:
                        w.last("pe", ("o", CH - 1, NT - 1))
                    last = copy(kv[0][:], kv_sum[:])
                elif kind == "oT":
                    if s[1]:
                        w.on("pe", ("y", s[1] - 1, 1))
                    else:
                        w.last("pe", ("y", CH - 1, 1))
                    last = copy(oT[0][:, s[2], :], src)
                elif kind == "foT":
                    w.last("pe", ("yf", 1))
                    last = copy(foT[0][:], src)
                elif kind == "E":
                    _, i, hp = s
                    w.on("dve", ("S", i, hp))
                    slot = units.index((i, hp)) % 2
                    for j in range(2):
                        at = sc[:, slot, j, 0:(i + 1) * P]
                        last = copy(at, at, ACT.Exp, bias=sbias[:, slot, j:j + 1], scale=FD ** -0.5)
                elif kind == "T":
                    _, i, hp, j = s
                    n = units.index((i, hp))
                    if n >= 2:
                        w.on("pe", ("AV", *units[n - 2]))
                    else:
                        w.last("pe", ("AV", *units[n - 2]))
                    last = copy(pT[0][:, n % 2, j, 0:(i + 1) * P], src[:, 0:(i + 1) * P])
                last.then_inc(act_steps, 1)

            act.sem_inc(act_steps, nbody["act"])
            act.wait_ge(const_in, 16)
            act.wait_ge(constants, 9)
            w.start()
            for s in START:
                if takes_part("act", s):
                    step(s, start_bank)
            with act.Fori(0, HALVES) as h:
                w.half(h)
                w.event = h * (B + 1)
                w.ended("pe")
                for s in PRE:
                    if takes_part("act", s):
                        step(s, pre_bank)
                with act.Fori(0, B) as b:
                    w.batch(b)
                    w.event = h * (B + 1) + b + 1
                    for s in BODY:
                        if takes_part("act", s):
                            step(s, ring_bank)

        @block.vector
        def _(dve):
            w = Waits(dve, "dve")
            linked = [0]

            def link(ins, alone=False):
                linked[0] += 1
                ins.then_inc(dve_link, 1)
                wait(dve, dve_link, w.links + linked[0], w.alone if alone else None)

            def rest(out, src, hi):
                return nc.vector.tensor_tensor(out, src, hi.bitcast(F32), ALU.subtract)

            def step(s, table):
                kind = s[0]
                if takes_part("act", s) and kind not in ("ln0", "S"):
                    w.on("act", s)
                elif takes_part("pe", s):
                    w.on("pe", s, alone=kind == "S")
                if kind not in NO_RING and takes_part("pe", s):
                    src = bank(s, table)
                if kind == "W":
                    dst = (Wq, Wk, Wv, Wo)[s[1]]
                    last = rest(dst[1][:].rearrange("p c n -> p (c n)"), staged[s[1] % 2],
                                dst[0][:].rearrange("p c n -> p (c n)"))
                elif kind == "wf":
                    dst = (Fq, Fk, Fv, Fo)[s[1]]
                    last = rest(dst[1][:], src[:, 0:D] if s[1] == 3 else src[:, 0:D].rearrange("p (c n) -> p c n", c=DC), dst[0][:])
                elif kind == "ln0":
                    if table is start_bank:
                        dve.wait_ge(first_x_in, 16)
                    else:
                        dve.wait_ge(x_in, 16 * w.tokens)
                    w.last("pool", ("ln1",), alone=True)
                    for t in range(NT):
                        ins = nc.vector.bn_stats(stats[:, t, :], xin[:, t, :])
                    link(ins, alone=True)
                    for t in range(NT):
                        ins = nc.vector.bn_aggr(moments[:, t, :], stats[:, t, :])
                    link(ins)
                    link(nc.vector.tensor_scalar(squares[:, 0, :], moments[:, :, 1], EPS, None, ALU.add))
                    last = nc.vector.scalar_tensor_tensor(squares[:, 1, :], squares[:, 0, :], EPS, moments[:, :, 1],
                                                          ALU.mult, ALU.add)
                elif kind == "ln1":
                    w.on("act", ("ln0",))
                    last = nc.vector.reciprocal(scales[:], roots[:])
                    if table is start_bank:
                        link(last)
                        for t in range(NT):
                            for n, out in enumerate((xn, xn2)):
                                last = nc.vector.tensor_scalar(out[:, t, :], xin[:, t, :], moments[:, t, 0:1],
                                                               scales[:, n, t:t + 1], ALU.subtract, ALU.mult)
                elif kind == "xT":
                    last = rest(xT[1][:, s[1], :], src, xT[0][:, s[1], :])
                elif kind == "x2T":
                    last = nc.vector.scalar_tensor_tensor(x2T[1][:, s[1], :], src, w1[:, s[1]:s[1] + 1],
                                                          x2T[0][:, s[1], :].bitcast(F32), ALU.mult, ALU.subtract)
                elif kind in ("qf", "kf"):
                    parts_of = fqk[kind == "kf"]
                    last = rest(parts_of[1][:], src, parts_of[0][:])
                elif kind == "vf":
                    heads = [vf[:, :, :, a, 0:FD] for a in range(PARTS)]
                    rest_h = vrest[:].rearrange("p t (h d) -> p t h d", h=GH)
                    link(nc.vector.tensor_tensor(rest_h, src.rearrange("p (t h d) -> p t h d", t=NT, h=GH), heads[0], ALU.subtract))
                    link(nc.vector.tensor_copy(heads[1], rest_h))
                    last = nc.vector.tensor_tensor(heads[2], rest_h, heads[1], ALU.subtract)
                elif kind == "k":
                    at = slice(2 * s[2], 2 * s[2] + 2)
                    last = nc.vector.scalar_tensor_tensor(k[1][:, at, :], src.rearrange("p (t n) -> p t n", t=2), 0.0,
                                                          k[0][:, at, :].bitcast(F32), ALU.max, ALU.subtract)
                elif kind == "v":
                    at = slice(2 * s[2], 2 * s[2] + 2)
                    last = rest(v[1][:, at, :, 0:LD], src.rearrange("p (t h d) -> p t h d", t=2, h=HC), v[0][:, at, :, 0:LD])
                elif kind == "q":
                    last = nc.vector.scalar_tensor_tensor(q[1][:, s[2], :], src, 0.0, q[0][:, s[2], :].bitcast(F32),
                                                          ALU.max, ALU.subtract)
                elif kind == "kv":
                    if s[2] == 0 and s[1]:
                        w.on("dve", ("kh", s[1] - 1))
                    elif s[2] == 0:
                        w.last("dve", ("kh", CH - 1))
                    for n in range(2):
                        rows, at = slice(LD * n, LD * (n + 1)), VW * n
                        last = nc.vector.tensor_tensor(kv_sum[rows, s[2], at:at + VW], src[rows, at:at + VW],
                                                       kv_rest[rows, s[2], at:at + VW], ALU.add)
                elif kind == "kh":
                    last = rest(kv[1][:], kv_sum[:], kv[0][:])
                elif kind == "o":
                    t = s[2]
                    if s[1]:
                        w.on("pe", ("oT", s[1] - 1, 1))
                    else:
                        w.last("pe", ("oT", CH - 1, 1))
                    heads = src[:, 0:HC * VW].rearrange("p (h n) -> p h n", h=HC)
                    link(nc.vector.tensor_scalar(norm[:, t % 2, :], heads[:, :, LD], 1e-06, None, ALU.max))
                    link(nc.vector.reciprocal(rnorm[:, t % 2, :], norm[:, t % 2, :]))
                    last = nc.vector.tensor_tensor(o[:, t, :].rearrange("p (h d) -> p h d", h=HC), heads[:, :, 0:LD],
                                                   rnorm[:, t % 2, :].unsqueeze(2).to_broadcast([P, HC, LD]), ALU.mult)
                elif kind == "oT":
                    last = rest(oT[1][:, s[2], :], src, oT[0][:, s[2], :])
                elif kind == "y":
                    at = yl[:, 2 * s[2]:2 * s[2] + 2, :]
                    new = src.rearrange("p (t n) -> p t n", t=2)
                    if s[1] == 0:
                        w.last("pool", STORED)
                        last = nc.vector.tensor_copy(at, new)
                    else:
                        w.on("dve", ("y", s[1] - 1, s[2]))
                        last = nc.vector.tensor_tensor(at, new, at, ALU.add)
                elif kind == "S":
                    _, i, hp = s
                    n = units.index((i, hp))
                    slot = n % 2
                    if n >= 2:
                        w.on("pe", ("T", *units[n - 2], 1), alone=True)
                    else:
                        w.last("pe", ("T", *units[n - 2], 1), alone=True)
                    for j in range(2):
                        ins = nc.vector.tensor_tensor_reduce(sc[:, slot, j, 0:(i + 1) * P], scores[:, j, 0:(i + 1) * P],
                                                             mask[:, S - (i + 1) * P:S], 1.0, MASKED, ALU.add, ALU.max,
                                                             smax[:, slot, j:j + 1])
                    link(ins)
                    last = nc.vector.tensor_scalar(sbias[:, slot, :], smax[:, slot, :], -FD ** -0.5, None, ALU.mult)
                elif kind == "T":
                    _, i, hp, j = s
                    slot = units.index((i, hp)) % 2
                    last = nc.vector.tensor_tensor(pT[1][:, slot, j, 0:(i + 1) * P], src[:, 0:(i + 1) * P],
                                                   pT[0][:, slot, j, 0:(i + 1) * P], ALU.subtract)
                elif kind == "AV":
                    _, i, _ = s
                    if i == NT - 1:
                        w.last("pe", ("foT",))
                    link(nc.vector.tensor_reduce(fsum[:], mixed[:, 0:GH * FV].rearrange("p (h a d) -> p h d a", h=GH, a=PARTS),
                                                 AX.X, ALU.add))
                    link(nc.vector.reciprocal(frec[:], fsum[:, :, FD]))
                    last = nc.vector.tensor_tensor(fo[:, i, :].rearrange("p (h d) -> p h d", h=GH), fsum[:, :, 0:FD],
                                                   frec[:].unsqueeze(2).to_broadcast([P, GH, FD]), ALU.mult)
                elif kind == "foT":
                    last = rest(foT[1][:], src, foT[0][:])
                elif kind == "yf":
                    if s[1] == 0:
                        w.last("pool", STORED)
                    last = nc.vector.tensor_copy(yf[:, 2 * s[1]:2 * s[1] + 2, :], src.rearrange("p (t n) -> p t n", t=2))
                last.then_inc(dve_steps, 1)

            def links(steps):
                return sum({"ln0": 3, "vf": 2, "o": 2, "S": 1, "AV": 2}.get(s[0], 0)
                           for s in steps if takes_part("dve", s))

            dve.sem_inc(dve_steps, nbody["dve"])
            dve.wait_ge(const_in, 16)
            dve.wait_ge(constants, 9)
            w.start()
            w.tokens, w.links, start_links = 0, 0, links(START) + 1
            for s in START:
                if takes_part("dve", s):
                    step(s, start_bank)
            with dve.Fori(0, HALVES) as h:
                w.half(h)
                w.links, linked[0] = start_links + h * (links(PRE) + B * links(BODY)), 0
                w.ended("pe")
                for s in PRE:
                    if takes_part("dve", s):
                        step(s, pre_bank)
                assert linked[0] == links(PRE)
                with dve.Fori(0, B) as b:
                    w.batch(b)
                    w.b = b
                    w.tokens = h * B + b + 1
                    w.links, linked[0] = start_links + h * (links(PRE) + B * links(BODY)) + links(PRE) + b * links(BODY), 0
                    for s in BODY:
                        if takes_part("dve", s):
                            step(s, ring_bank)
                    assert linked[0] == links(BODY)


PREP = [("prep", m, j) for m in "gud" for j in range(2)]
EXPERT = [("cw",), ("g", 0), ("u", 0), ("g", 1), ("u", 1), ("h", 0), ("g", 2), ("u", 2), ("h", 1), ("d", 0),
          ("h", 2), ("g", 3), ("u", 3), ("d", 1), ("h", 3), ("d", 2), ("d", 3)]
ROUTE = [("norm", 1), ("norm", 2), ("mT", 0), ("mT", 1), ("norm", 0), ("logits",), ("tokens",), ("top",), ("weights",)]
FIRST_ROUTE = [("first",)] + ROUTE
BOTH = [("cw",), ("g", 0), ("u", 0), ("g", 1), ("h", 0), ("u", 1), ("g", 2), ("norm", 1), ("d", 0), ("u", 2),
        ("h", 1), ("g", 3), ("norm", 2), ("u", 3), ("d", 1), ("h", 2), ("h", 3), ("mT", 0), ("mT", 1), ("d", 2),
        ("d", 3), ("logits",), ("norm", 0), ("tokens",), ("top",), ("weights",)]
R3 = 6
PARTS_OF = {"prep": ("pe", "act", "dve"), "cw": ("dve",), "g": ("pe", "act"), "u": ("pe", "dve"), "h": ("act", "dve"),
            "d": ("pe", "dve"), "norm": ("act", "dve"), "first": ("act", "dve"), "mT": ("pe", "act", "dve"), "logits": ("pe", "dve"),
            "tokens": ("pe", "dve"), "top": ("act", "dve"), "weights": ("dve",)}


def takes(e, s):
    if s[0] == "norm" and s[1] == 2:
        return e == "dve"
    if s[0] == "d":
        return e == "pe" or e == "dve" and s[1] == IC - 1
    return e in PARTS_OF[s[0]]


def count(e, steps):
    return sum(takes(e, s) for s in steps)


def expert_phase(nc, x, bo, linear_in, softmax_in, w_ln2, wr, wg, wu, wd, out):
    engines = ("pe", "act", "dve")
    start = {e: count(e, PREP + FIRST_ROUTE + PREP) for e in engines}
    n_both = {e: count(e, BOTH) for e in engines}
    n_expert = {e: count(e, EXPERT) for e in engines}
    n_prep = {e: count(e, PREP) for e in engines}
    AHEAD = dict(n_both)
    after_first = {e: start[e] + (B - 1) * n_both[e] + n_expert[e] for e in engines}
    one_expert = {e: n_prep[e] + B * n_expert[e] for e in engines}
    index_of = {}
    for name, steps in (("prep", PREP), ("route", FIRST_ROUTE), ("both", BOTH), ("expert", EXPERT)):
        index_of[name] = {e: {s: n for n, s in enumerate([s for s in steps if takes(e, s)])} for e in engines}

    def expert_start(ex):
        return {e: after_first[e] + ex * one_expert[e] - B * n_expert[e] for e in engines}

    with ExitStack() as ctx:
        def sb(name, shape, dt=F32):
            return ctx.enter_context(nc.sbuf_tensor(name, shape, dt))

        def parts(name, shape):
            return [sb(f"{name}_hi", shape, F32R), sb(f"{name}_lo", shape, F32R)]

        def sem(name):
            return ctx.enter_context(nc.semaphore(name))

        xmT = parts("xmT", [P, DC, B * S])
        acc = sb("acc", [P, B * NT, D])
        WgT = [parts(f"WgT{n}", [P, DC, I]) for n in range(2)]
        WuT = [parts(f"WuT{n}", [P, DC, I]) for n in range(2)]
        WdT = [parts(f"WdT{n}", [P, IC, D]) for n in range(2)]
        raw = {"g": sb("raw_g", [P, IC, D]), "u": sb("raw_u", [P, IC, D]), "d": sb("raw_d", [P, DC, I])}
        WrT = parts("WrT", [P, DC, P])
        raw_r = sb("raw_r", [P, DC, E])
        identity = sb("identity", [P, P])
        w2 = sb("w2", [P, D])
        bias = sb("bias", [P, D])
        silu = sb("silu", [P, 2, S])
        h = sb("h", [P, 2, S])
        hT = parts("hT", [P, IC, S])
        cw = sb("cw", [P, E, B * NT])
        cw_now = sb("cw_now", [P, NT])
        xt = sb("xt", [P, NT, D])
        lin = sb("lin", [P, 2, NT, D])
        sof = sb("sof", [P, 2, NT, D])
        logitsT = sof[:, 1].rearrange("p t d -> p (t d)")[:, 0:S]
        stats = sb("stats3", [P, NT, 6])
        moments = sb("moments3", [P, NT, 2])
        small = sb("small", [P, 10, NT])
        var_eps, std, rstd, ms_eps, rms, rrms, gap, expgap, p0, p1 = (small[:, n, :] for n in range(10))
        logits = sb("logits", [P, NT, E])
        top = sb("top", [P, NT, 8])
        top_at = sb("top_at", [P, NT, 8], U32)
        top_f = sb("top_f", [P, NT, 8])
        experts = sb("experts", [P, NT, E])
        chosen = sb("chosen", [P, 2, NT, E])

        ring = ctx.enter_context(nc.psum_tensor("ring3", [P, R3, 512], F32))
        down = ctx.enter_context(nc.psum_tensor("down", [P, 2, 512], F32))

        progress = {"pe": sem("pe_steps3"), "act": sem("act_steps3"), "dve": sem("dve_steps3")}
        pool_steps = sem("pool_steps3")
        dve_link = sem("dve_link3")
        constants = sem("constants3")
        const_in = sem("const_in3")
        raw_in = sem("raw_in")
        x_in, linear_in_sbuf, softmax_in_sbuf = sem("x_in3"), sem("linear_in_sbuf"), sem("softmax_in_sbuf")
        stored = sem("stored")

        class Waits:
            def __init__(self, eng, me):
                self.eng = eng
                self.alone = (eng.alloc_register(f"{me}_waited_for3"), constants)

            def enter(self, table, base):
                self.table, self.index, self.base, self.seen = table, index_of[table], base, {}

            def at(self, e, n, alone=False):
                if self.seen.get(e, -10**9) < n:
                    self.seen[e] = n
                    wait(self.eng, progress[e], self.base[e] + AHEAD[e] + n, self.alone if alone else None)

            def on(self, e, step, alone=False):
                self.at(e, self.index[e][step] + 1, alone)

            def last(self, e, step, alone=False):
                self.at(e, self.index[e][step] + 1 - len(self.index[e]), alone)

            def before(self, e):
                self.at(e, 0)

        def ring_jobs(table):
            steps = {"both": BOTH, "expert": EXPERT, "route": ROUTE}[table]
            return [s for s in steps if takes("pe", s) and s[0] != "d"]

        def bank(table, s):
            return ring[:, ring_jobs(table).index(s) % R3, :]

        def prep_bank(s):
            return ring[:, PREP.index(s), :]

        def freed_by(s):
            return ("u", s[1]) if s[0] == "g" else s

        def ring_free(w, s):
            jobs = ring_jobs(w.table)
            n = jobs.index(s)
            if n >= R3:
                w.on("dve", freed_by(jobs[n - R3]))
            elif w.table == "route":
                w.before("dve")
            else:
                step = freed_by([j for m, j in enumerate(jobs) if m % R3 == n][-1])
                w.at("dve", max(w.index["dve"][step] + 1 - len(w.index["dve"]), n + 1 - len(PREP)))

        def run(w, me, step, fori):
            def steps(table, base, what, **at):
                w.enter(table, base)
                for s in what:
                    if takes(me, s):
                        step(s, w, **at)

            zero = {e: 0 for e in engines}
            w.fresh = True
            steps("prep", zero, PREP, nxt=0, parity=0)
            steps("route", {e: n_prep[e] for e in engines}, FIRST_ROUTE, to=0)
            steps("prep", {e: n_prep[e] + count(e, FIRST_ROUTE) for e in engines}, PREP, nxt=1, parity=1)
            with fori(0, B - 1) as n:
                steps("both", {e: start[e] + n * n_both[e] for e in engines}, BOTH, n=n, ex=0, parity=0, to=n + 1)
            w.fresh = False
            if me == "pe":
                w.enter("expert", {e: after_first[e] - n_expert[e] for e in engines})
                w.before("dve")
            steps("expert", {e: after_first[e] - n_expert[e] for e in engines}, EXPERT, n=B - 1, ex=0, parity=0)
            with fori(0, (E - 2) // 2) as pair:
                for k in range(2):
                    ex = 2 * pair + 1 + k
                    base = expert_start(ex)
                    steps("prep", {e: base[e] - n_prep[e] for e in engines}, PREP, nxt=ex + 1, parity=k)
                    with fori(0, B) as n:
                        steps("expert", {e: base[e] + n * n_expert[e] for e in engines}, EXPERT, n=n, ex=ex, parity=1 - k)
            base = {e: expert_start(E - 1)[e] - n_prep[e] for e in engines}
            with fori(0, B) as n:
                steps("expert", {e: base[e] + n * n_expert[e] for e in engines}, EXPERT, n=n, ex=E - 1, parity=1)

        block = ctx.enter_context(nc.Block())

        @block.gpsimd
        def _(pool):
            pool.memset(identity[:], 0.0).then_inc(constants, 1)
            for part in WrT:
                pool.memset(part[:].bitcast(F32), 0.0).then_inc(constants, 1)
            pool.wait_ge(constants, 3)
            pool.affine_select(out=identity[:], in_=identity[:], compare_op=ALU.not_equal, fill=1.0, base=0,
                               pattern=[[-1, P]], channel_multiplier=1).then_inc(constants, 1)
            pool.iota(experts[:], pattern=[[0, NT], [1, E]], base=0, channel_multiplier=0,
                      allow_small_or_imprecise_dtypes=True).then_inc(constants, 1)
            pool.wait_ge(const_in, 64)
            def add_up(n, normalised):
                pool.wait_ge(x_in, 16 * n + 16)
                pool.wait_ge(linear_in_sbuf, 32 * n + 32)
                nc.gpsimd.tensor_tensor(lin[:, 0], lin[:, 0], lin[:, 1], ALU.add).then_inc(pool_steps, 1)
                pool.wait_ge(pool_steps, 5 * n + 1)
                nc.gpsimd.tensor_tensor(lin[:, 0], lin[:, 0], xt[:], ALU.add).then_inc(pool_steps, 1)
                pool.wait_ge(softmax_in_sbuf, 32 * n + 32)
                nc.gpsimd.tensor_tensor(sof[:, 0], sof[:, 0], sof[:, 1], ALU.add).then_inc(pool_steps, 1)
                pool.wait_ge(pool_steps, 5 * n + 2)
                nc.gpsimd.tensor_tensor(lin[:, 0], lin[:, 0], bias[:].unsqueeze(1).to_broadcast([P, NT, D]),
                                        ALU.add).then_inc(pool_steps, 1)
                pool.wait_ge(progress["dve"], AHEAD["dve"] + normalised)
                pool.wait_ge(pool_steps, 5 * n + 4)
                nc.gpsimd.tensor_tensor(acc[:, bass.ds(NT * n, NT), :], lin[:, 0], sof[:, 0], ALU.add).then_inc(pool_steps, 1)

            add_up(0, n_prep["dve"] + index_of["route"]["dve"]["norm", 1] + 1)
            with pool.Fori(0, B - 1) as n:
                add_up(n + 1, start["dve"] + n * n_both["dve"] + index_of["both"]["dve"]["norm", 1] + 1)

        @block.sync
        def _(sp):
            def rows(m):
                return m.rearrange("(t p) d -> p t d", p=P)

            def load_weights(ex):
                sp.dma_start(raw["g"][:], rows(wg[ex])).then_inc(raw_in, 16)
                sp.dma_start(raw["u"][:], rows(wu[ex])).then_inc(raw_in, 16)
                sp.dma_start(raw["d"][:], rows(wd[ex])).then_inc(raw_in, 16)

            def load_tokens(n, table, base):
                def ended(e, step):
                    if table:
                        wait(sp, progress[e], AHEAD[e] + base[e] + index_of[table][e][step] + 1, alone)

                ended("dve", ("norm", 1))
                sp.dma_start(xt[:], rows(x[n])).then_inc(x_in, 16)
                if table:
                    wait(sp, pool_steps, 5 * n, alone)
                for k in range(HALVES):
                    sp.dma_start(lin[:, k], rows(linear_in[k, n])).then_inc(linear_in_sbuf, 16)
                ended("dve", ("norm", 2))
                sp.dma_start(sof[:, 0], rows(softmax_in[0, n])).then_inc(softmax_in_sbuf, 16)
                ended("pe", ("tokens",))
                sp.dma_start(sof[:, 1], rows(softmax_in[1, n])).then_inc(softmax_in_sbuf, 16)

            sp.wait_ge(constants, 1)
            alone = (sp.alloc_register("sp_waited_for3"), constants)
            sp.dma_start(w2[:], w_ln2.partition_broadcast(P)).then_inc(const_in, 16)
            sp.dma_start(bias[:], bo.partition_broadcast(P)).then_inc(const_in, 16)
            for c in range(DC):
                sp.dma_start(raw_r[:, c, :], wr[:, c * P:(c + 1) * P].rearrange("e p -> p e"), allow_slow_non_contiguous=True)\
                    .then_inc(const_in, 16)
            load_weights(0)
            load_tokens(0, None, None)
            wait(sp, progress["pe"], AHEAD["pe"] + n_prep["pe"], alone)
            load_weights(1)
            load_tokens(1, "route", n_prep)
            wait(sp, progress["pe"], AHEAD["pe"] + start["pe"], alone)
            load_weights(2)
            with sp.Fori(0, B - 2) as n:
                load_tokens(n + 2, "both", {e: start[e] + n * n_both[e] for e in engines})
            wait(sp, progress["dve"], AHEAD["dve"] + start["dve"] + (B - 2) * n_both["dve"] + index_of["both"]["dve"]["norm", 1] + 1)
            sp.dma_start(xt[:], rows(x[0])).then_inc(x_in, 16)
            with sp.Fori(3, E) as ex:
                wait(sp, progress["pe"], AHEAD["pe"] + after_first["pe"] + (ex - 3) * one_expert["pe"] + n_prep["pe"], alone)
                load_weights(ex)
            with sp.Fori(0, B) as n:
                wait(sp, progress["dve"], AHEAD["dve"] + expert_start(E - 1)["dve"] - n_prep["dve"] + (n + 1) * n_expert["dve"], alone)
                sp.dma_start(rows(out[n]), acc[:, bass.ds(NT * n, NT), :]).then_inc(stored, 16)
            sp.wait_ge(stored, 16 * B)
            sp.wait_ge(x_in, 16 * (B + 1))

        @block.tensor
        def _(pe):
            w = Waits(pe, "pe")

            def products(out, left, right, blocks):
                pairs = [(c, a, b) for c in range(blocks) for a, b in PRODUCTS]
                for m, (c, a, b) in enumerate(pairs):
                    last = nc.tensor.matmul(out, left(a, c), right(b, c), start=m == 0, stop=m == len(pairs) - 1)
                return last

            def step(s, w, n=None, ex=None, parity=None, to=None, nxt=None):
                kind = s[0]
                if kind not in ("prep", "d"):
                    ring_free(w, s)
                    dst = bank(w.table, s)
                if kind == "prep":
                    job = PREP.index(s)
                    if job == 0:
                        pe.wait_ge(raw_in, 48 * nxt + 48)
                        w.at("dve", 0 if w.fresh else index_of["expert"]["dve"]["u", IC - 1] + 1 - n_expert["dve"])
                    dst = prep_bank(s)
                    for m in range(4):
                        if s[1] == "d":
                            src = raw["d"][:, m % 2, (2 * s[2] + m // 2) * P:(2 * s[2] + m // 2 + 1) * P]
                        else:
                            src = raw[s[1]][:, m, s[2] * P:(s[2] + 1) * P]
                        last = nc.tensor.transpose(dst[:, m * P:(m + 1) * P], src, identity[:])
                elif kind in ("g", "u"):
                    weights = (WgT if kind == "g" else WuT)[parity]
                    at = bass.ds(S * n, S)
                    last = products(dst, lambda a, c: weights[a][:, c, s[1] * P:(s[1] + 1) * P],
                                    lambda b, c: xmT[b][:, c, at], DC)
                elif kind == "d":
                    ic = s[1]
                    w.on("dve", ("h", ic))
                    if ic == 0:
                        w.before("dve")
                    for t in range(NT):
                        for m, (a, b) in enumerate(PRODUCTS):
                            last = nc.tensor.matmul(down[:, t // 2, (t % 2) * D:(t % 2 + 1) * D], hT[a][:, ic, t * P:(t + 1) * P],
                                                    WdT[parity][b][:, ic, :], start=ic == 0 and m == 0 and t % 2 == 0,
                                                    stop=ic == IC - 1 and m == 2, skip_group_check=True)
                elif kind == "mT":
                    w.on("dve", ("norm", 2))
                    for t in range(NT):
                        last = nc.tensor.transpose(dst[:, t * P:(t + 1) * P], sof[:, 1, t, s[1] * P:(s[1] + 1) * P], identity[:])
                elif kind == "logits":
                    w.on("dve", ("mT", 1))
                    last = products(dst, lambda a, c: WrT[a][:, c, :], lambda b, c: xmT[b][:, c, bass.ds(S * to, S)], DC)
                elif kind == "tokens":
                    w.on("dve", ("logits",))
                    for t in range(NT):
                        last = nc.tensor.transpose(dst[:, t * P:(t + 1) * P], logitsT[:, t * P:(t + 1) * P], identity[:])
                last.then_inc(progress["pe"], 1)

            pe.sem_inc(progress["pe"], AHEAD["pe"])
            pe.wait_ge(constants, 7)
            run(w, "pe", step, pe.Fori)

        @block.scalar
        def _(act):
            w = Waits(act, "act")

            def copy(out, in_, func=ACT.Copy):
                return nc.scalar.activation(out, in_, func)

            def step(s, w, n=None, ex=None, parity=None, to=None, nxt=None):
                kind = s[0]
                if kind in ("prep", "g", "mT"):
                    w.on("pe", s)
                if kind == "prep":
                    dst = {"g": WgT, "u": WuT, "d": WdT}[s[1]][parity][0]
                    if s[1] == "d":
                        last = copy(dst[:, 2 * s[2]:2 * s[2] + 2, :], prep_bank(s).rearrange("p (c n) -> p c n", c=2))
                    else:
                        last = copy(dst[:, s[2], :], prep_bank(s))
                elif kind == "g":
                    if s[1] >= 2:
                        w.on("dve", ("u", s[1] - 2))
                    else:
                        w.last("dve", ("u", s[1] + 2))
                    last = copy(silu[:, s[1] % 2, :], bank(w.table, s), ACT.Silu)
                elif kind == "h":
                    w.on("dve", ("u", s[1]))
                    w.last("pe", ("d", s[1]))
                    last = copy(hT[0][:, s[1], :], h[:, s[1] % 2, :])
                elif kind in ("norm", "first"):
                    w.on("dve", s)
                    last = copy(rms, ms_eps, ACT.Sqrt) if s == ("norm", 1) else copy(std, var_eps, ACT.Sqrt)
                elif kind == "mT":
                    last = copy(xmT[0][:, s[1], bass.ds(S * to, S)], bank(w.table, s))
                elif kind == "top":
                    w.on("dve", s)
                    last = copy(expgap, gap, ACT.Exp)
                last.then_inc(progress["act"], 1)

            act.sem_inc(progress["act"], AHEAD["act"])
            act.wait_ge(const_in, 64)
            act.wait_ge(constants, 5)
            nc.scalar.activation(WrT[0][:, :, 0:E], raw_r[:], ACT.Copy).then_inc(constants, 1)
            run(w, "act", step, act.Fori)

        @block.vector
        def _(dve):
            w = Waits(dve, "dve")
            linked = [0]
            LINKS = {"norm": {0: 2, 1: 3, 2: 1}, "logits": {None: 0}, "top": {None: 4}, "weights": {None: 6}}

            def links(steps):
                return sum(LINKS[s[0]][s[1] if len(s) > 1 else None] for s in steps if s[0] in LINKS)

            def link(ins, alone=False):
                linked[0] += 1
                ins.then_inc(dve_link, 1)
                wait(dve, dve_link, w.links + linked[0], w.alone if alone else None)

            def rest(out, src, hi):
                return nc.vector.tensor_tensor(out, src, hi.bitcast(F32), ALU.subtract)

            def step(s, w, n=None, ex=None, parity=None, to=None, nxt=None):
                kind = s[0]
                if s == ("first",):
                    w.links = 0
                elif s == ROUTE[0]:
                    w.links, linked[0] = LINKS["norm"][0] + to * links(ROUTE), 0
                if kind in ("prep", "mT", "h"):
                    w.on("act", s)
                elif kind in ("u", "d", "logits", "tokens"):
                    w.on("pe", s)
                if kind == "prep":
                    dst = {"g": WgT, "u": WuT, "d": WdT}[s[1]][parity]
                    src = prep_bank(s)
                    if s[1] == "d":
                        at = slice(2 * s[2], 2 * s[2] + 2)
                        last = rest(dst[1][:, at, :], src.rearrange("p (c n) -> p c n", c=2), dst[0][:, at, :])
                    else:
                        last = rest(dst[1][:, s[2], :], src, dst[0][:, s[2], :])
                elif kind == "cw":
                    w.before("dve")
                    last = nc.vector.tensor_copy(cw_now[:], cw[:, ex, bass.ds(NT * n, NT)])
                elif kind == "u":
                    w.on("act", ("g", s[1]))
                    if s[1] >= 2:
                        w.on("act", ("h", s[1] - 2))
                        w.on("dve", ("h", s[1] - 2))
                    else:
                        w.last("act", ("h", s[1] + 2))
                        w.last("dve", ("h", s[1] + 2))
                    last = nc.vector.tensor_tensor(h[:, s[1] % 2, :], bank(w.table, s), silu[:, s[1] % 2, :], ALU.mult)
                elif kind == "h":
                    w.last("pe", ("d", s[1]))
                    last = rest(hT[1][:, s[1], :], h[:, s[1] % 2, :], hT[0][:, s[1], :])
                elif kind == "d":
                    w.on("dve", ("cw",))
                    for t in range(NT):
                        at = acc[:, bass.ds(NT * n + t, 1), :].rearrange("p o d -> p (o d)")
                        last = nc.vector.scalar_tensor_tensor(at, down[:, t // 2, (t % 2) * D:(t % 2 + 1) * D], cw_now[:, t:t + 1],
                                                              at, ALU.mult, ALU.add)
                elif s in (("first",), ("norm", 0)):
                    dve.wait_ge(x_in, 16 if kind == "first" else 16 * to + 32)
                    for t in range(NT):
                        ins = nc.vector.bn_stats(stats[:, t, :], xt[:, t, :])
                    link(ins, alone=True)
                    for t in range(NT):
                        ins = nc.vector.bn_aggr(moments[:, t, :], stats[:, t, :])
                    link(ins)
                    last = nc.vector.tensor_scalar(var_eps, moments[:, :, 1], EPS, None, ALU.add)
                elif s == ("norm", 1):
                    if w.table == "route":
                        w.on("act", ("first",))
                    else:
                        w.last("act", ("norm", 0))
                    link(nc.vector.reciprocal(rstd, std))
                    dve.wait_ge(pool_steps, 5 * to + 3)
                    for t in range(NT):
                        ins = nc.vector.tensor_scalar(xt[:, t, :], xt[:, t, :], moments[:, t, 0:1], rstd[:, t:t + 1],
                                                      ALU.subtract, ALU.mult)
                    link(ins)
                    link(nc.vector.tensor_tensor(sof[:, 0], sof[:, 0], xt[:], ALU.add))
                    for t in range(NT):
                        last = nc.vector.tensor_tensor_reduce(sof[:, 1, t, :], sof[:, 0, t, :], sof[:, 0, t, :], 1.0 / D, EPS,
                                                              ALU.mult, ALU.add, ms_eps[:, t:t + 1])
                elif s == ("norm", 2):
                    w.on("act", ("norm", 1))
                    w.on("dve", ("norm", 1))
                    link(nc.vector.reciprocal(rrms, rms))
                    for t in range(NT):
                        last = nc.vector.scalar_tensor_tensor(sof[:, 1, t, :], sof[:, 0, t, :], rrms[:, t:t + 1], w2[:],
                                                              ALU.mult, ALU.mult)
                elif kind == "mT":
                    src = bank(w.table, s)
                    last = rest(xmT[1][:, s[1], bass.ds(S * to, S)], src, xmT[0][:, s[1], bass.ds(S * to, S)])
                elif kind == "logits":
                    w.on("pe", ("mT", 1))
                    last = nc.vector.tensor_copy(logitsT, bank(w.table, s))
                elif kind == "tokens":
                    last = nc.vector.tensor_copy(logits[:], bank(w.table, s).rearrange("p (t n) -> p t n", t=NT)[:, :, 0:E])
                elif kind == "top":
                    w.on("dve", ("tokens",), alone=True)
                    for t in range(NT):
                        ins = nc.vector.max(top[:, t, :], logits[:, t, :])
                    link(ins, alone=True)
                    for t in range(NT):
                        ins = nc.vector.max_index(top_at[:, t, :], top[:, t, :], logits[:, t, :])
                    link(ins)
                    link(nc.vector.tensor_copy(top_f[:], top_at[:]))
                    link(nc.vector.tensor_tensor(gap, top[:, :, 1], top[:, :, 0], ALU.subtract))
                    for k in range(2):
                        last = nc.vector.tensor_tensor(chosen[:, k], experts[:], top_f[:, :, k].unsqueeze(2).to_broadcast([P, NT, E]),
                                                       ALU.is_equal)
                elif kind == "weights":
                    w.on("act", ("top",))
                    w.on("dve", ("top",))
                    link(nc.vector.tensor_scalar(p1, expgap, 1.0, None, ALU.add))
                    link(nc.vector.reciprocal(p0, p1))
                    link(nc.vector.tensor_tensor(p1, expgap, p0, ALU.mult))
                    for k, pk in enumerate((p0, p1)):
                        link(nc.vector.tensor_tensor(chosen[:, k], chosen[:, k], pk.unsqueeze(2).to_broadcast([P, NT, E]), ALU.mult))
                    link(nc.vector.tensor_tensor(chosen[:, 0], chosen[:, 0], chosen[:, 1], ALU.add))
                    dve.wait_ge(pool_steps, 5 * to + 5)
                    last = nc.vector.tensor_copy(cw[:, :, bass.ds(NT * to, NT)], chosen[:, 0].rearrange("p t e -> p e t"))
                last.then_inc(progress["dve"], 1)

            dve.sem_inc(progress["dve"], AHEAD["dve"])
            dve.wait_ge(constants, 6)
            rest(WrT[1][:, :, 0:E], raw_r[:], WrT[0][:, :, 0:E]).then_inc(constants, 1)
            run(w, "dve", step, dve.Fori)
            assert linked[0] == links(ROUTE), (linked[0], links(ROUTE))


_INS = ["L0_attn_hidden_states", "L0_attn_Wq", "L0_attn_Wk", "L0_attn_Wv", "L0_attn_Wo", "L0_attn_bo",
        "L0_ffn_Wq", "L0_ffn_Wk", "L0_ffn_Wv", "L0_ffn_Wo", "L0_ffn_w_ln1", "L0_ffn_w_ln2",
        "L0_ffn_Wr", "L0_ffn_Wg", "L0_ffn_Wu", "L0_ffn_Wd"]


def program(nc, x, wq, wk, wv, wo, bo, fwq, fwk, fwv, fwo, w_ln1, w_ln2, wr, wg, wu, wd, out):
    linear_parts = nc.dram_tensor("linear_parts", [HALVES, B, S, D], F32, kind="Internal").ap()
    softmax_parts = nc.dram_tensor("softmax_parts", [HALVES, B, S, D], F32, kind="Internal").ap()
    stack_store = nc.dram_tensor("stack_store", [2, 2, P, S], F32, kind="Internal").ap()
    attention_phase(nc, x, wq, wk, wv, wo, fwq, fwk, fwv, fwo, w_ln1, linear_parts, softmax_parts, stack_store)
    expert_phase(nc, x, bo, linear_parts, softmax_parts, w_ln2, wr, wg, wu, wd, out)


def kernel(**inputs):
    import concourse.bacc as bacc
    from concourse.bass_utils import run_bass_kernel_spmd

    nc = bacc.Bacc("TRN2", target_bir_lowering=False, num_devices=1)
    arrays, args = {}, []
    for name in _INS:
        array = np.ascontiguousarray(inputs[name])
        arrays[f"in_{name}"] = array
        args.append(nc.dram_tensor(f"in_{name}", array.shape, mybir.dt.from_np(array.dtype), kind="ExternalInput").ap())
    out = nc.dram_tensor("out", [B, S, D], F32, kind="ExternalOutput").ap()
    program(nc, *args, out)
    result = run_bass_kernel_spmd(nc, [arrays], core_ids=[0])
    return result.results[0]["out"]
```
